# Optimizing a Trainium2 kernel written in Bass

```python
import numpy as np
import jax
import jax.numpy as jnp

def _softmax(x, axis=-1):
    return jax.nn.softmax(x, axis=axis)

def _gelu(x):
    return jax.nn.gelu(x, approximate=True)

def _silu(x):
    return jax.nn.silu(x)

def _sigmoid(x):
    return jax.nn.sigmoid(x)

def _layernorm(x, axis=-1, eps=1e-05):
    m = jnp.mean(x, axis=axis, keepdims=True)
    v = jnp.var(x, axis=axis, keepdims=True)
    return (x - m) / jnp.sqrt(v + eps)

def _scatter_add(tgt, idx, src, axis=0):
    return tgt.at[idx].add(src)

def _segment_sum(src, seg, n):
    return jax.ops.segment_sum(src, seg, n)
kernel_name = 'mk_sandwich_d1_jaxref_r4_8cb6d6'

def setup_inputs(seed: int=0):
    np.random.seed(seed)
    _w = jnp.asarray

    def _L0_attn_setup():
        import jax, jax.numpy as jnp
        import numpy as np
        B, S, H, NH, MRP = (4, 256, 256, 16, 64)
        DK = H // NH
        VOCAB = 2 * MRP + 1

        def _rel_idx(seq_len):
            r = jnp.arange(seq_len)
            dist = r[None, :] - r[:, None]
            return jnp.clip(dist, -MRP, MRP) + MRP
        key = jax.random.key(seed)
        ks = jax.random.split(key, 12)
        sc = 1.0 / np.sqrt(H)
        inp = {'x': jax.random.normal(ks[0], (B, S, H), jnp.float32), 'mask': jnp.ones((B, S), jnp.int32), 'Wq': jax.random.normal(ks[1], (H, H), jnp.float32) * sc, 'bq': jnp.zeros((H,), jnp.float32), 'Wk': jax.random.normal(ks[2], (H, H), jnp.float32) * sc, 'bk': jnp.zeros((H,), jnp.float32), 'Wv': jax.random.normal(ks[3], (H, H), jnp.float32) * sc, 'bv': jnp.zeros((H,), jnp.float32), 'Wo': jax.random.normal(ks[4], (H, H), jnp.float32) * sc, 'bo': jnp.zeros((H,), jnp.float32), 'embK': jax.random.normal(ks[5], (VOCAB, DK), jnp.float32), 'embV': jax.random.normal(ks[6], (VOCAB, DK), jnp.float32)}
        return inp
    _L0_attn_in = _L0_attn_setup()

    def _L0_ffn_setup():
        import jax, jax.numpy as jnp
        import numpy as np
        THRESH_FACTOR = 0.7

        def ternary_quantize(w):
            delta = THRESH_FACTOR * jnp.mean(jnp.abs(w))
            return jnp.where(w > delta, 1.0, jnp.where(w < -delta, -1.0, 0.0)).astype(w.dtype)
        key = jax.random.key(seed)
        k1, k2, k3 = jax.random.split(key, 3)
        B, S, D_IN, D_OUT = (8, 1024, 256, 256)
        inp = {'input': jax.random.normal(k1, (B, S, D_IN), dtype=jnp.float32), 'weight': jax.random.normal(k2, (D_OUT, D_IN), dtype=jnp.float32) * (1.0 / np.sqrt(D_IN)), 'alpha': jnp.ones((1,), dtype=jnp.float32), 'bias': jax.random.normal(k3, (D_OUT,), dtype=jnp.float32) * (1.0 / np.sqrt(D_IN))}
        return inp
    _L0_ffn_in = _L0_ffn_setup()
    _d = {'L0_attn_x': _L0_attn_in['x'], 'L0_attn_mask': _L0_attn_in['mask'], 'L0_attn_Wq': _L0_attn_in['Wq'], 'L0_attn_bq': _L0_attn_in['bq'], 'L0_attn_Wk': _L0_attn_in['Wk'], 'L0_attn_bk': _L0_attn_in['bk'], 'L0_attn_Wv': _L0_attn_in['Wv'], 'L0_attn_bv': _L0_attn_in['bv'], 'L0_attn_Wo': _L0_attn_in['Wo'], 'L0_attn_bo': _L0_attn_in['bo'], 'L0_attn_embK': _L0_attn_in['embK'], 'L0_attn_embV': _L0_attn_in['embV'], 'L0_ffn_weight': _L0_ffn_in['weight'], 'L0_ffn_alpha': _L0_ffn_in['alpha'], 'L0_ffn_bias': _L0_ffn_in['bias']}
    _x0 = _d['L0_attn_x']
    _d['L0_attn_x'] = jax.random.normal(jax.random.fold_in(jax.random.key(seed), 1), (8, 1024, 256), dtype=_x0.dtype)
    del _x0
    return _d

def reference(L0_attn_x, L0_attn_mask, L0_attn_Wq, L0_attn_bq, L0_attn_Wk, L0_attn_bk, L0_attn_Wv, L0_attn_bv, L0_attn_Wo, L0_attn_bo, L0_attn_embK, L0_attn_embV, L0_ffn_weight, L0_ffn_alpha, L0_ffn_bias):

    def _L0_attn_ref(x, mask, Wq, bq, Wk, bk, Wv, bv, Wo, bo, embK, embV):
        import jax, jax.numpy as jnp
        import numpy as np
        B, S, H, NH, MRP = (4, 256, 256, 16, 64)
        DK = H // NH
        VOCAB = 2 * MRP + 1

        def _rel_idx(seq_len):
            r = jnp.arange(seq_len)
            dist = r[None, :] - r[:, None]
            return jnp.clip(dist, -MRP, MRP) + MRP
        nb, seq_len, _ = x.shape
        idx = _rel_idx(seq_len)
        rk = embK[idx]
        rv = embV[idx]

        def proj(W, b):
            return (x @ W.T + b).reshape(nb, seq_len, NH, DK).transpose(0, 2, 1, 3)
        q = proj(Wq, bq)
        k = proj(Wk, bk)
        v = proj(Wv, bv)
        logits = jnp.einsum('bhqd,bhkd->bhqk', q, k) + jnp.einsum('bhqd,qkd->bhqk', q, rk)
        w = jax.nn.softmax(logits, axis=-1)
        out = jnp.einsum('bhqk,bhkd->bhqd', w, v) + jnp.einsum('bhqk,qkd->bhqd', w, rv)
        out = out.transpose(0, 2, 1, 3).reshape(nb, seq_len, NH * DK)
        return out @ Wo.T + bo

    def _L0_ffn_ref(input, weight, alpha, bias):
        import jax, jax.numpy as jnp
        import numpy as np
        THRESH_FACTOR = 0.7

        def ternary_quantize(w):
            delta = THRESH_FACTOR * jnp.mean(jnp.abs(w))
            return jnp.where(w > delta, 1.0, jnp.where(w < -delta, -1.0, 0.0)).astype(w.dtype)
        w_ternary = ternary_quantize(weight)
        w_eff = w_ternary * alpha
        out = jnp.einsum('bsd,od->bso', input, w_eff) + bias
        return out
    x = L0_attn_x
    x = x + _layernorm(_L0_attn_ref(_layernorm(x, axis=-1), L0_attn_mask, L0_attn_Wq, L0_attn_bq, L0_attn_Wk, L0_attn_bk, L0_attn_Wv, L0_attn_bv, L0_attn_Wo, L0_attn_bo, L0_attn_embK, L0_attn_embV), axis=-1)
    x = x + _layernorm(_L0_ffn_ref(_layernorm(x, axis=-1), L0_ffn_weight, L0_ffn_alpha, L0_ffn_bias), axis=-1)
    return x

_drawn_inputs = setup_inputs


def setup_inputs(seed=0):
    import zlib

    import numpy as np

    out = dict(_drawn_inputs(seed))
    spreads = {'L0_attn_bq': (0.0, 0.1),
     'L0_attn_bk': (0.0, 0.8),
     'L0_attn_bv': (0.0, 0.1),
     'L0_attn_bo': (0.0, 0.1)}
    factors = {'L0_ffn_bias': 8.0}
    for name, (base, spread) in spreads.items():
        noise = np.random.default_rng([zlib.crc32(name.encode()), seed]).standard_normal(out[name].shape)
        drawn = base * np.exp(spread * noise) if base else spread * noise
        out[name] = jnp.asarray(drawn.astype(out[name].dtype))
    for name, factor in factors.items():
        out[name] = (out[name] * factor).astype(out[name].dtype)
    return out
```

```python
from contextlib import ExitStack

import numpy as np
import concourse.bass as bass
from concourse import mybir

F32 = mybir.dt.float32
BF16 = mybir.dt.bfloat16
ALU = mybir.AluOpType
ACT = mybir.ActivationFunctionType
AX = mybir.AxisListType

P = 128
B, S, H = 8, 1024, 256
NH, D, MRP = 16, 16, 64
VOCAB = 2 * MRP + 1
T = S // P
G = 2
HG = NH // G
STEPS = B * G * T
QPARTS = (0, 1, 2, 0, 1, 0)
KPARTS = (0, 0, 0, 1, 1, 2)
NB = len(QPARTS)
SPLIT = NB * D
FAR = SPLIT + 3
ROWS = FAR + 2
QDROWS = SPLIT + 6
CHUNK = 2
NCHUNK = T // CHUNK
CT = CHUNK * P
WIN = 2 * P
HALF = P // 2
FW, GW = P, HALF
PW = FW + GW
SLOT = WIN + HALF
VW = D + 1
QG = 8
NQG = P // QG
EXT = P + WIN - 1
EPS = 1e-5
LOWEST = -3.0e38
QRING, BRING, VRING = 4, 3, 3


class Sem:

    def __init__(self, handle):
        self.handle, self.value = handle, 0

    def up(self, n):
        self.value += n
        return (self, self.value)


class Queue:

    def __init__(self, done):
        self.items, self.done, self.seen = [], done, {}

    def wait(self, after):
        for sem, value in after:
            if self.seen.get(sem, 0) < value:
                self.seen[sem] = value
                self.items.append(lambda e, s=sem.handle, v=value: e.wait_ge(s, v))

    def do(self, f, after=(), signal=True):
        self.wait(after)
        if signal:
            tok = self.done.up(1)
            self.items.append(lambda e: f(e).then_inc(self.done.handle, 1))
            return tok
        self.items.append(f)
        return None

    def dma(self, out, in_, sem, after=()):
        self.wait(after)
        tok = sem.up(16)
        self.items.append(lambda e: e.dma_start(out, in_).then_inc(sem.handle, 16))
        return tok

    def run(self, engine):
        for f in self.items:
            f(engine)


def tile_layout(t):
    band = [k for k in (t - 1, t, t + 1) if 0 <= k < T]
    rest = [k for k in range(T) if k not in band]
    x = band + rest[:4 - len(band)]
    return x, rest[4 - len(band):]


def score_pieces(t):
    first = max(P * t - HALF, 0)
    runs = []
    for c in range(0, S, HALF):
        k = (c + first) % S
        side = "L" if k < P * t else "C" if k < P * t + P else "R"
        if runs and c % 512 and runs[-1][3] == side and runs[-1][1] + runs[-1][2] == k:
            runs[-1][2] += HALF
        else:
            runs.append([c, k, HALF, side])
    return runs


def window(t):
    width = WIN if 0 < t < T - 1 else WIN - HALF
    return width, HALF + (HALF if t == 0 else 0)


def build(nc, a, out):
    ctx = ExitStack()
    with ctx:
        def sb(name, shape, dt=F32):
            return ctx.enter_context(nc.sbuf_tensor(name, shape, dt))

        def ps(name, cols):
            return ctx.enter_context(nc.psum_tensor(name, [P, cols], F32))

        def sem(name):
            return Sem(ctx.enter_context(nc.semaphore(name)))

        scores = ps("scores", S)
        logitsT = [ps(f"logitsT{i}", 512) for i in range(3)]
        oacc = ps("oacc", 512)
        misc = [ps(f"misc{i}", 512) for i in range(2)]

        ident = sb("ident", [P, P])
        ones = sb("ones", [P, P])
        wq, wk, wv, wo, wf = (sb(n, [P, 2, H]) for n in ("wq", "wk", "wv", "wo", "wf"))
        bq, bk = sb("bq", [P, G]), sb("bk", [P, G])
        vbase = sb("vbase", [P, 2, H])
        bo, bf = sb("bo", [P, H]), sb("bf", [P, H])
        alpha = sb("alpha", [P, 1])
        relmask, relsum = sb("relmask", [P, QG]), sb("relsum", [P, D])
        headmask, kfar = sb("headmask", [P, HG]), sb("kfar", [P, 2])
        farw = sb("farw", [P, 2, HG])
        partmask = sb("partmask", [SPLIT, 3])
        embk6 = sb("embk6", [SPLIT, VOCAB])
        bandtab = [sb(f"bandtab{i}", [SPLIT, PW], BF16) for i in range(2)]
        reltab = sb("reltab", [P, WIN, D])
        relbase = sb("relbase", [P, 2, D])
        small = sb("small", [P, 8])

        ks = [sb(f"ks{i}", [ROWS, HG, S], BF16) for i in range(2)]
        ql = [sb(f"ql{i}", [ROWS, HG, P], BF16) for i in range(QRING)]
        qr = [sb(f"qr{i}", [ROWS, HG, P], BF16) for i in range(QRING)]
        vl = [sb(f"vl{i}", [P, T, HG, VW]) for i in range(VRING)]
        vr = [sb(f"vr{i}", [P, T, HG, VW]) for i in range(VRING)]
        band = [sb(f"band{i}", [P, HG * SLOT + HALF]) for i in range(BRING)]
        praw = sb("praw", [P, HG, PW])
        wx = sb("wx", [P, HG, 512])
        wy = sb("wy", [P, 4, 512])
        junk = [sb(f"junk{i}", [P, WIN], BF16) for i in range(2)]
        maxes = [sb(f"maxes{i}", [P, HG, 3]) for i in range(2)]
        negmax = [sb(f"negmax{i}", [P, HG]) for i in range(2)]
        nmT = sb("nmT", [HG, P])
        nm1, nm2 = sb("nm1", [HG, P], BF16), sb("nm2", [HG, P], BF16)
        relout = sb("relout", [P, 2, 512])
        oT = sb("oT", [P, 2, P])
        rsum = sb("rsum", [P, HG])
        attn = sb("attn", [P, T, H])
        xc = sb("xc", [P, CHUNK, H])
        xnT = sb("xnT", [P, 2, CT])
        qf = sb("qf", [P, G, CT])
        qres = sb("qres", [P, G, CT])
        qp = [sb(f"qp{i}", [P, G, CT], BF16) for i in range(3)]
        fp = [sb(f"fp{i}", [2 * HG, G, CT], BF16) for i in range(3)]
        attT, x1T = sb("attT", [P, 2, P]), sb("x1T", [P, 2, P])
        vb_raw = attT[:].rearrange("p i t -> p (i t)")
        xt = [sb(f"xt{i}", [P, H]) for i in range(2)]
        ybuf = [sb(f"ybuf{i}", [P, H]) for i in range(2)]
        x1 = [sb(f"x1_{i}", [P, H]) for i in range(2)]
        xn1 = sb("xn1", [P, H])
        zbuf = [sb(f"zbuf{i}", [P, H]) for i in range(2)]
        stats = [sb(f"stats{i}", [P, CHUNK, 6]) for i in range(3)]
        mv = [sb(f"mv{i}", [P, CHUNK, 2]) for i in range(3)]
        rs = [sb(f"rs{i}", [P, 5, CHUNK]) for i in range(3)]

        qd = [nc.dram_tensor(f"qd{i}", [G, QDROWS, HG, S], BF16).ap() for i in range(2)]
        kd = [nc.dram_tensor(f"kd{i}", [G, SPLIT, HG, S], BF16).ap() for i in range(2)]
        FP_, GP_ = 2 * P, P
        fs = [nc.dram_tensor(f"fs{i}", [HG, P, FP_], F32) for i in range(2)]
        gs = [nc.dram_tensor(f"gs{i}", [HG, P, GP_], F32) for i in range(2)]
        nmd = [nc.dram_tensor(f"nmd{i}", [2, HG, P], BF16).ap() for i in range(2)]

        PE = Queue(sem("pe_done"))
        DVE = Queue(sem("dve_done"))
        ACTQ = Queue(sem("act_done"))
        POOL = Queue(sem("pool_done"))
        SP = Queue(sem("sp_done"))
        s_const, s_zero, s_x = sem("s_const"), sem("s_zero"), sem("s_x")
        s_chunk = {w: [[sem(f"s_{w}{i}_{c}") for c in range(NCHUNK)] for i in range(2)] for w in ("qd", "far", "kd")}
        s_ks = [[sem(f"s_ks{i}_{c}") for c in range(NCHUNK)] for i in range(2)]
        s_q = [sem(f"s_q{i}") for i in range(QRING)]
        s_nmw, s_nm = [sem(f"s_nmw{i}") for i in range(2)], [sem(f"s_nm{i}") for i in range(2)]
        s_bw, s_br = [sem(f"s_bw{i}") for i in range(2)], [sem(f"s_br{i}") for i in range(BRING)]
        s_xt, s_out = [sem(f"s_xt{i}") for i in range(2)], [sem(f"s_out{i}") for i in range(2)]

        def load(dst, src):
            return SP.dma(dst, src, s_const)

        for t_, n in ((wq, "WqT"), (wk, "WkT"), (wv, "WvT"), (wo, "WoT"), (wf, "WfT")):
            load(t_[:], a[n].rearrange("(i p) o -> p i o", p=P))
        for t_, n in ((ident, "ident"), (bq, "bq"), (bk, "bk"), (relmask, "relmask"), (relsum, "relsum"),
                      (headmask, "headmask"), (kfar, "kfar"), (partmask, "partmask"), (embk6, "embk6")):
            load(t_[:], a[n])
        for t_, n in ((vb_raw, "bv"), (bo[:], "bo"), (bf[:], "bf"), (alpha[:], "alpha")):
            load(t_, a[n].partition_broadcast(P))
        load(vbase[:], a["efarV"].partition_broadcast(P))
        load(relbase[:], a["relbase"].partition_broadcast(P))
        ext = a["extV"]
        consts = load(reltab[:].rearrange("p n d -> p (n d)"), bass.AP(ext.tensor, 0, [[D, P], [1, WIN * D]]))

        ones_set = POOL.do(lambda e: e.memset(ones[:], 1.0))
        cleared = []
        for t_ in band:
            cleared.append(POOL.do(lambda e, t_=t_: e.memset(t_[:], 0.0)))
        zero_src = band[0][:, 0:FP_]
        zeroed = []
        for i in range(2):
            for dst, w in ((fs[i], FP_), (gs[i], GP_)):
                for h in range(HG):
                    zeroed.append(SP.dma(dst.ap()[h], zero_src[:, 0:w], s_zero, [cleared[0]]))
        zeroed = [zeroed[-1]]
        for t_ in vl + vr:
            DVE.do(lambda e, t_=t_: e.memset(t_[:, :, :, D:VW], 1.0))
        for t_ in ks:
            DVE.do(lambda e, t_=t_: e.memset(t_[SPLIT:ROWS, :, :], 1.0))
        v_ones = DVE.do(lambda e: e.memset(oacc[:], 0.0))
        reltab_ready = None
        for i in range(2):
            hp = P * i
            reltab_ready = POOL.do(lambda e, i=i, hp=hp: e.tensor_tensor(
                reltab[:, hp:hp + P, :], reltab[:, hp:hp + P, :],
                relbase[:, i:i + 1, :].broadcast_to([P, P, D]), ALU.subtract), [consts])
        vbase_ready = None
        for i in range(2):
            vbase_ready = POOL.do(lambda e, i=i: e.tensor_tensor(vbase[:, i, :], vbase[:, i, :], vb_raw, ALU.add),
                                  [consts])
        for i in range(2):
            farw_ready = DVE.do(lambda e, i=i: e.tensor_scalar(farw[:, i, :], headmask[:], kfar[:, i:i + 1], None,
                                                               ALU.mult), [consts])
        bt_f, bt_p = ybuf[1], ybuf[0]
        jobs = [(0, 0, FW, 0, VOCAB - 1), (0, FW, GW, 0, 0), (1, 0, FW, 0, 0), (1, FW, GW, HALF, VOCAB - 1)]
        for tab, c, n, r, base in jobs:
            prev = DVE.do(lambda e, c=c, n=n, r=r, base=base: e.tensor_scalar(
                bt_f[0:SPLIT, c:c + n], embk6[:, r:r + n], embk6[:, base:base + 1], None, ALU.subtract),
                [consts, (DVE.done, DVE.done.value)])
            if c == 0:
                continue
            for part in range(3):
                prev = DVE.do(lambda e, tab=tab: e.tensor_copy(qp[0][0:SPLIT, 0, 0:PW], bt_f[0:SPLIT, 0:PW]), [prev])
                keep = bandtab[tab]
                if part == 0:
                    prev = DVE.do(lambda e, k=keep: e.tensor_scalar(
                        bt_p[0:SPLIT, 0:PW], qp[0][0:SPLIT, 0, 0:PW], partmask[:, 0:1], None, ALU.mult), [prev])
                else:
                    prev = DVE.do(lambda e, i=part: e.scalar_tensor_tensor(
                        bt_p[0:SPLIT, 0:PW], qp[0][0:SPLIT, 0, 0:PW], partmask[:, i:i + 1],
                        bt_p[0:SPLIT, 0:PW], ALU.mult, ALU.add), [prev])
                prev = DVE.do(lambda e: e.tensor_tensor(bt_f[0:SPLIT, 0:PW], bt_f[0:SPLIT, 0:PW],
                                                        qp[0][0:SPLIT, 0, 0:PW], ALU.subtract), [prev])
            tab_ready = DVE.do(lambda e, k=keep: e.tensor_copy(k[:, :], bt_p[0:SPLIT, 0:PW]), [prev])
        prev = DVE.do(lambda e: e.tensor_reduce(small[:, 0:1], wf[:], AX.XY, ALU.add, apply_absolute_value=True), [consts])
        prev = PE.do(lambda e: e.matmul(misc[0][:, 0:1], ones[:], small[:, 0:1], start=True, stop=True),
                     [prev, ones_set])
        prev = DVE.do(lambda e: e.tensor_scalar(small[:, 1:2], misc[0][:, 0:1], 1.0 / (H * H), 0.7, ALU.mult, ALU.mult), [prev])
        prev = DVE.do(lambda e: e.tensor_scalar(small[:, 2:3], small[:, 1:2], -1.0, None, ALU.mult), [prev])
        above, below = zbuf[0], zbuf[1]
        for i in range(2):
            DVE.do(lambda e, i=i: e.tensor_scalar(above[:], wf[:, i, :], small[:, 1:2], None, ALU.is_gt), [prev])
            prev = DVE.do(lambda e, i=i: e.tensor_scalar(below[:], wf[:, i, :], small[:, 2:3], None, ALU.is_lt), [prev])
            prev = DVE.do(lambda e, i=i: e.tensor_tensor(above[:], above[:], below[:], ALU.subtract), [prev])
            wf_ready = prev = DVE.do(lambda e, i=i: e.tensor_scalar(wf[:, i, :], above[:], alpha[:, 0:1], None, ALU.mult), [prev])

        bank = {"n": 0, "free": [wf_ready, v_ones]}

        def small_bank():
            i = bank["n"] % 2
            bank["n"] += 1
            return i, misc[i], bank["free"][i]

        def freed(i, tok):
            bank["free"][i] = tok

        ln_used = [[] for _ in range(3)]

        def inv_std(k, srcs, after):
            n = len(srcs)
            r = rs[k]
            for i, s_ in enumerate(srcs):
                prev = DVE.do(lambda e, s_=s_, i=i: e.bn_stats(stats[k][:, i, :], s_), after + ln_used[k])
            for i in range(n):
                prev = DVE.do(lambda e, i=i: e.bn_aggr(mv[k][:, i, :], stats[k][:, i, :]), [prev])
            prev = DVE.do(lambda e: e.tensor_scalar(r[:, 0, 0:n], mv[k][:, 0:n, 1], EPS, None, ALU.add), [prev])
            prev = ACTQ.do(lambda e: e.activation(r[:, 1, 0:n], r[:, 0, 0:n], ACT.Ln), [prev])
            prev = ACTQ.do(lambda e: e.activation(r[:, 2, 0:n], r[:, 1, 0:n], ACT.Exp, scale=-0.5), [prev])
            prev = POOL.do(lambda e: e.tensor_tensor(r[:, 3, 0:n], r[:, 0, 0:n], r[:, 2, 0:n], ALU.mult), [prev])
            prev = POOL.do(lambda e: e.tensor_tensor(r[:, 3, 0:n], r[:, 3, 0:n], r[:, 2, 0:n], ALU.mult), [prev])
            prev = POOL.do(lambda e: e.tensor_scalar(r[:, 3, 0:n], r[:, 3, 0:n], -0.5, 1.5, ALU.mult, ALU.add), [prev])
            prev = POOL.do(lambda e: e.tensor_tensor(r[:, 4, 0:n], r[:, 3, 0:n], r[:, 2, 0:n], ALU.mult), [prev])
            return prev

        def normed(q, k, i, dst, src, after):
            tok = q.do(lambda e: e.tensor_scalar(dst, src, mv[k][:, i, 0:1], rs[k][:, 4, i:i + 1],
                                                 ALU.subtract, ALU.mult), after)
            ln_used[k] = [tok]
            return tok

        xrow = a["x"].rearrange("(b c i p) h -> b c p i h", b=B, c=NCHUNK, i=CHUNK)
        st = {"xc": [], "xnT": [], "qf": [], "qp": [], "fp": [], "qres": []}
        q_loaded, k_loaded, v_written, v_read = {}, {}, {}, {}
        chunk_written = {}

        def prep(b, c):
            buf = b % 2
            loc = {}

            def stage0():
                got = SP.dma(xc[:], xrow[b, c], s_x, st["xc"])
                r = inv_std(0, [xc[:, i, :] for i in range(CHUNK)], [got])
                for i in range(CHUNK):
                    loc["xn"] = normed(POOL, 0, i, xc[:, i, :], xc[:, i, :], [r])

            def stage1():
                i_, m, free = small_bank()
                for ih in range(2):
                    for i in range(CHUNK):
                        tr = PE.do(lambda e, ih=ih, i=i, m=m: e.matmul(
                            m[:, ih * CT + i * P:ih * CT + (i + 1) * P], xc[:, i, ih * P:(ih + 1) * P], ident[:],
                            start=True, stop=True, is_transpose=True), [loc["xn"], free, consts])
                st["xc"] = [tr]
                loc["xnT"] = ACTQ.do(lambda e, m=m: e.activation(xnT[:].rearrange("p i t -> p (i t)"), m[:, 0:2 * CT],
                                                                ACT.Copy), [tr] + st["xnT"])
                freed(i_, loc["xnT"])

            def project(w, bias, parts, dram, rows, name):
                i_, m, free = small_bank()
                for g in range(G):
                    for ih in range(2):
                        mm = PE.do(lambda e, g=g, ih=ih, m=m: e.matmul(
                            m[:, g * CT:(g + 1) * CT], w[:, ih, g * P:(g + 1) * P], xnT[:, ih, :],
                            start=ih == 0, stop=ih == 1), [loc["xnT"], free], signal=ih == 1)
                for g in range(G):
                    ev = ACTQ.do(lambda e, g=g, m=m: e.activation(qf[:, g, :], m[:, g * CT:(g + 1) * CT], ACT.Identity,
                                                                  bias=bias[:, g:g + 1]), [mm] + st["qf"])
                freed(i_, ev)
                src, after = qf, [ev] + st["qp"]
                for k in range(3):
                    cp = POOL.do(lambda e, src=src, k=k: e.tensor_copy(qp[k][:], src[:]), after)
                    if k < 2:
                        sub = POOL.do(lambda e, src=src, k=k: e.tensor_tensor(qres[:], src[:], qp[k][:], ALU.subtract),
                                      [cp] + st["qres"])
                        src, after = qres, [sub]
                st["qf"], st["qres"] = [sub], [cp]
                s_ = s_chunk[name][buf][c]
                old = chunk_reads(b - 2)
                for r, k in enumerate(parts):
                    w_ = POOL.dma(bass.AP(dram[buf].tensor, r * D * HG * S + c * CT,
                                          [[S, P], [rows * HG * S, G], [1, CT]]), qp[k][:], s_, [cp] + old)
                st["qp"] = [w_]
                chunk_written.setdefault((b, c), []).append(w_)
                return ev

            def stage2():
                loc["q"] = project(wq, bq, QPARTS, qd, QDROWS, "qd")

            def stage2b():
                i_, m, free = small_bank()
                mm = PE.do(lambda e, m=m: e.matmul(m[0:2 * HG, 0:G * CT], farw[:].rearrange("p a h -> p (a h)"),
                                                   qf[:].rearrange("p g t -> p (g t)"), start=True, stop=True),
                           [loc["q"], farw_ready, free])
                st["qf"] = st["qf"] + [mm]
                fv = qres[0:2 * HG, :, :]
                ev = DVE.do(lambda e, m=m: e.tensor_copy(fv.rearrange("p g t -> p (g t)"), m[0:2 * HG, 0:G * CT]),
                            [mm] + st["qres"])
                freed(i_, ev)
                prev = ev
                for k in range(3):
                    cp = POOL.do(lambda e, k=k: e.tensor_copy(fp[k][:], fv), [prev] + st["fp"])
                    if k < 2:
                        prev = POOL.do(lambda e, k=k: e.tensor_tensor(fv, fv, fp[k][:], ALU.subtract), [cp])
                st["qres"] = [cp]
                s_ = s_chunk["far"][buf][c]
                for k in range(3):
                    w_ = POOL.dma(bass.AP(qd[buf].tensor, (SPLIT + 2 * k) * HG * S + c * CT,
                                          [[S, 2 * HG], [QDROWS * HG * S, G], [1, CT]]), fp[k][:], s_, [cp])
                st["fp"] = [w_]
                chunk_written[b, c].append(w_)

            def stage3():
                project(wk, bk, KPARTS, kd, SPLIT, "kd")

            def stage4():
                i_, m, free = small_bank()
                for i in range(CHUNK):
                    for ih in range(2):
                        mm = PE.do(lambda e, i=i, ih=ih, m=m: e.matmul(
                            m[:, i * H:(i + 1) * H], xnT[:, ih, i * P:(i + 1) * P], wv[:, ih, :],
                            start=ih == 0, stop=ih == 1), [loc["xnT"], free], signal=ih == 1)
                st["xnT"] = [mm]
                for side, ring in enumerate((vl, vr)):
                    for g in range(G):
                        n = b * G + g
                        ev = DVE.do(lambda e, side=side, ring=ring, g=g, n=n, m=m: e.tensor_tensor(
                            ring[n % VRING][:, c * CHUNK:(c + 1) * CHUNK, :, 0:D].rearrange("p i h d -> p i h d"),
                            m[:, 0:CHUNK * H].rearrange("p (i g h d) -> p g i h d", i=CHUNK, g=G, h=HG)[:, g],
                            vbase[:, side:side + 1, g * P:(g + 1) * P].rearrange("p a (h d) -> p a h d", h=HG)
                            .broadcast_to([P, CHUNK, HG, D]), ALU.add),
                            [mm, vbase_ready] + v_read.get(n - VRING, []))
                        v_written[n] = [ev]
                freed(i_, ev)
            return [stage0, stage1, stage2, stage2b, stage3, stage4]

        def chunk_reads(b):
            if b < 0:
                return []
            return [q_loaded[s] for s in range(b * G * T, (b + 1) * G * T)][-QRING:] + \
                   [k_loaded[b * G + g, c] for g in range(G) for c in range(NCHUNK)]

        tok = {}

        def get(*key):
            return [tok[key]] if key in tok else []

        def load_k(n):
            b, g = divmod(n, G)
            for c in range(NCHUNK):
                k_loaded[n, c] = SP.dma(ks[n % 2][0:SPLIT, :, c * CT:(c + 1) * CT], kd[b % 2][g, :, :, c * CT:(c + 1) * CT],
                                        s_ks[n % 2][c], chunk_written[b, c] + [v_ones] + get("st_done", (n - 1) * T - 1))

        def load_q(s):
            n, t = divmod(s, T)
            b, g = divmod(n, G)
            i = s % QRING
            after = chunk_written[b, t // CHUNK] + get("st_done", s - QRING)
            src = qd[b % 2][g]
            for side, q_ in enumerate((ql[i], qr[i])):
                SP.dma(q_[0:SPLIT, :, :], src[0:SPLIT, :, t * P:(t + 1) * P], s_q[i], after)
                q_loaded[s] = SP.dma(q_[SPLIT:FAR, :, :],
                                     bass.AP(src.tensor, src.offset + (SPLIT + side) * HG * S + t * P,
                                             [[2 * HG * S, 3], [S, HG], [1, P]]), s_q[i], after)

        def band_raw(s, pair):
            i = s % QRING
            i_, m, free = small_bank()
            for j in range(2):
                h = 2 * pair + j
                for half in range(2):
                    mm = PE.do(lambda e, h=h, j=j, half=half, m=m: e.matmul(
                        m[HALF * half:HALF * (half + 1), j * PW:(j + 1) * PW],
                        ql[i][0:SPLIT, h, HALF * half:HALF * (half + 1)], bandtab[half][:], start=True, stop=True),
                        [q_loaded[s], tab_ready, free], signal=j == 1)
            ev = ACTQ.do(lambda e, m=m: e.activation(praw[:, 2 * pair:2 * pair + 2, :].rearrange("p h c -> p (h c)"),
                                                     m[:, 0:2 * PW], ACT.Copy), [mm] + get("bw", s - 1))
            freed(i_, ev)
            tok["praw", s] = ev

        def band_write(s):
            k = s % 2
            for half in range(2):
                rows = slice(HALF * half, HALF * (half + 1))
                f0, g0 = (0, HALF) if half == 0 else (P, 0)
                after = [tok["praw", s]] + zeroed + get("br", s - 2)
                SP.dma(fs[k].ap()[:, rows, f0:f0 + FW].rearrange("h p c -> p h c"), praw[rows, :, 0:FW], s_bw[k], after)
                tok["bw", s] = SP.dma(gs[k].ap()[:, rows, g0:g0 + GW].rearrange("h p c -> p h c"),
                                      praw[rows, :, FW:PW], s_bw[k], after)

        def band_read(s):
            k, i = s % 2, s % BRING
            slots = band[i][:, 0:HG * SLOT].rearrange("p (h c) -> p h c", h=HG)
            after = [tok["bw", s], cleared[-1]] + get("st_done", s - BRING)
            for half in range(2):
                rows = slice(HALF * half, HALF * (half + 1))
                flo, glo = (HALF + HALF, HALF) if half == 0 else (HALF, HALF + WIN - HALF)
                SP.dma(slots[rows, :, flo:flo + WIN - HALF],
                       bass.AP(fs[k], HALF * half * FP_ + HALF, [[FP_ - 1, HALF], [P * FP_, HG], [1, WIN - HALF]]),
                       s_br[i], after)
                tok["br", s] = SP.dma(slots[rows, :, glo:glo + HALF],
                                      bass.AP(gs[k], HALF * half * GP_ + HALF, [[GP_ - 1, HALF], [P * GP_, HG], [1, HALF]]),
                                      s_br[i], after)

        def row_max(s, h):
            n, t = divmod(s, T)
            i, k, mx = s % QRING, ks[n % 2], maxes[s % 2]
            first = True
            kin = [k_loaded[n, c] for c in range(NCHUNK)] if t == 0 and h == 0 else []
            u = s * HG + h
            for c, key, length, side in score_pieces(t):
                after = [q_loaded[s]] + kin + get("max", u - 1, c // 512)
                last = c + length in (512, S)
                if side == "C":
                    for half, q_ in ((0, qr[i]), (1, ql[i])):
                        r = slice(HALF * half, HALF * (half + 1))
                        mm = PE.do(lambda e, r=r, q_=q_, c=c, key=key, length=length: e.matmul(
                            scores[r, c:c + length], q_[0:FAR, h, r], k[0:FAR, h, key:key + length],
                            start=True, stop=True), after, signal=last and half == 1)
                else:
                    q_ = ql[i] if side == "L" else qr[i]
                    mm = PE.do(lambda e, q_=q_, c=c, key=key, length=length: e.matmul(
                        scores[:, c:c + length], q_[0:FAR, h, :], k[0:FAR, h, key:key + length],
                        start=True, stop=True), after, signal=last)
                if c + length == 512:
                    full0 = mm
            width, off = window(t)
            bcol = h * SLOT + off
            mxfree = get("negmax", s - 2)
            DVE.do(lambda e: e.tensor_tensor_reduce(
                junk[u % 2][:, 0:width], scores[:, 0:width], band[s % BRING][:, bcol:bcol + width], 1.0, LOWEST,
                ALU.add, ALU.max, mx[:, h, 0:1]), [full0, tok["br", s]] + mxfree + get("max", u - 1, 1) + [tab_ready])
            tok["max", u, 0] = DVE.do(lambda e: e.tensor_reduce(mx[:, h, 1:2], scores[:, width:512], AX.X, ALU.max))
            tok["max", u, 1] = DVE.do(lambda e: e.tensor_reduce(mx[:, h, 2:3], scores[:, 512:S], AX.X, ALU.max), [mm])

        def max_reduce(s):
            tok["negmax", s] = DVE.do(lambda e: e.tensor_reduce(negmax[s % 2][:], maxes[s % 2][:], AX.X, ALU.max, negate=True),
                                      [tok["max", s * HG + HG - 1, 1]] + get("nmT", s - 2))

        def max_rows(s):
            i_, m, free = small_bank()
            tr = PE.do(lambda e, m=m: e.matmul(m[0:HG, 0:P], negmax[s % 2][:], ident[:], start=True, stop=True,
                                               is_transpose=True), [tok["negmax", s], free])
            tok["nmT", s] = tr
            ev = DVE.do(lambda e, m=m: e.tensor_copy(nmT[:], m[0:HG, 0:P]), [tr] + get("nm2", s - 1))
            freed(i_, ev)
            c1 = POOL.do(lambda e: e.tensor_copy(nm1[:], nmT[:]), [ev] + get("nmw", s - 1))
            c2 = tok["nm2", s] = POOL.do(lambda e: e.tensor_tensor(nm2[:], nmT[:], nm1[:], ALU.subtract), [c1])
            k, i = s % 2, s % QRING
            after = [c2] + get("nm", s - 2)
            POOL.dma(nmd[k][0], nm1[:], s_nmw[k], after)
            w_ = tok["nmw", s] = POOL.dma(nmd[k][1], nm2[:], s_nmw[k], after)
            for q_ in (ql[i], qr[i]):
                tok["nm", s] = POOL.dma(q_[FAR:ROWS, :, :], nmd[k], s_nm[k], [w_] + get("st_done", s - QRING))

        bankT = {"n": 0}
        exp_tok = {}

        def weights(s, h, kind):
            n, t = divmod(s, T)
            i, k = s % QRING, ks[n % 2]
            tiles = tile_layout(t)[0 if kind == "X" else 1]
            j = bankT["n"] % 3
            bankT["n"] += 1
            m = logitsT[j]
            after = [tok["nm", s], q_loaded[s]] + get("exp", bankT["n"] - 4)
            for c, kt in enumerate(tiles):
                lhs = k[0:ROWS, h, kt * P:(kt + 1) * P]
                band_tile = kind == "X" and abs(kt - t) <= 1
                last = c == len(tiles) - 1
                if kt == t:
                    for half, q_ in ((0, qr[i]), (1, ql[i])):
                        mm = PE.do(lambda e, c=c, half=half, q_=q_, lhs=lhs: e.matmul(
                            m[:, c * P + HALF * half:c * P + HALF * (half + 1)], lhs,
                            q_[0:ROWS, h, HALF * half:HALF * (half + 1)], start=half == 0, stop=not band_tile,
                            skip_group_check=True), after, signal=False)
                else:
                    q_ = ql[i] if kt < t else qr[i]
                    mm = PE.do(lambda e, c=c, q_=q_, lhs=lhs: e.matmul(
                        m[:, c * P:(c + 1) * P], lhs, q_[0:ROWS, h, :], start=True, stop=not band_tile,
                        skip_group_check=True), after, signal=last and not band_tile)
                if band_tile:
                    bc = h * SLOT + (kt - t + 1) * P
                    mm = PE.do(lambda e, c=c, bc=bc: e.matmul(
                        m[:, c * P:(c + 1) * P], band[s % BRING][:, bc:bc + P], ident[:], start=False, stop=True,
                        is_transpose=True, skip_group_check=True), [tok["br", s]], signal=last)
            tok["st_done", s] = mm
            if kind == "X":
                dst, free = wx[:, h, :], get("rel", s - 1) + get("pvX", s - 1, h // 4)
            else:
                dst = wy[:, h % 4, :]
                free = get("pvY", s - 1, 1) if h < 4 else get("pvY", s, 0)
            e_ = ACTQ.do(lambda e: e.activation(dst, m[:], ACT.Exp), [mm] + free)
            tok["exp", bankT["n"] - 1] = e_
            exp_tok[s, h, kind] = e_

        def weighted(s, blk, kind):
            n, t = divmod(s, T)
            tiles = tile_layout(t)[0 if kind == "X" else 1]
            VL, VR = vl[n % VRING], vr[n % VRING]
            after = [exp_tok[s, 4 * blk + j, kind] for j in range(4)] + v_written[n]
            if blk == 0 and kind == "X":
                after = after + get("o_out", s - 1)
            for c, kt in enumerate(tiles):
                for half in ((0, 1) if kt == t else (None,)):
                    for j in range(4):
                        h = 4 * blk + j
                        V = VL if kt < t or half == 1 else VR
                        q0, qn = (0, P) if half is None else (HALF * half, HALF)
                        src = wx[:, h, :] if kind == "X" else wy[:, j, :]
                        start = blk == 0 and kind == "X" and c == 0 and half in (None, 0)
                        last = c == len(tiles) - 1 and half in (None, 1) and j == 3
                        mm = PE.do(lambda e, V=V, h=h, j=j, c=c, q0=q0, qn=qn, kt=kt, src=src, start=start: e.matmul(
                            oacc[32 * j:32 * j + VW, blk * P + q0:blk * P + q0 + qn], V[:, kt, h, :],
                            src[:, c * P + q0:c * P + q0 + qn], start=start, stop=True, skip_group_check=True),
                            after, signal=last)
            tok["pv" + kind, s, blk] = mm
            if kind == "Y" and blk == 1:
                v_read[n] = [mm]
                tok["pv_all", s] = mm

        def relative(s, part):
            t = s % T
            tiles = tile_layout(t)[0]
            i_, m, free = small_bank()
            after = [exp_tok[s, h, "X"] for h in range(HG)] + [free, reltab_ready]
            for gq in range(NQG // 2):
                q0 = (part * NQG // 2 + gq) * QG
                near = [kt for kt in ((t - 1, t) if q0 < HALF else (t, t + 1)) if 0 <= kt < T]
                for x, kt in enumerate(near):
                    n0 = P * (kt - t) - (q0 + QG - 1) + (EXT // 2)
                    c = tiles.index(kt) * P + q0
                    mm = PE.do(lambda e, n0=n0, c=c, gq=gq, x=x, m=m, near=near: e.matmul(
                        m[:, gq * HG * QG:(gq + 1) * HG * QG], reltab[:, n0:n0 + QG, :].rearrange("p n d -> p (n d)"),
                        wx[:, :, c:c + QG], start=x == 0, stop=x == len(near) - 1),
                        after, signal=gq == NQG // 2 - 1 and x == len(near) - 1)
            if part == 1:
                tok["rel", s] = mm
            ev = DVE.do(lambda e, m=m: e.tensor_tensor(
                relout[:, part, :].rearrange("p (a c) -> p a c", c=QG), m[:].rearrange("p (a c) -> p a c", c=QG),
                relmask[:].rearrange("p (a c) -> p a c", a=1).broadcast_to([P, 512 // QG, QG]), ALU.mult),
                [mm] + get("relsum", s - 1))
            freed(i_, ev)
            tok["relout", s] = ev

        def relative_sum(s):
            src = relout[:].rearrange("p a (g h c) -> p (a g) h c", h=HG, c=QG)
            for blk in range(2):
                for j in range(4):
                    h = 4 * blk + j
                    mm = PE.do(lambda e, h=h, j=j, blk=blk: e.matmul(
                        oacc[32 * j:32 * j + D, blk * P:(blk + 1) * P], relsum[:], src[:, :, h, :],
                        start=False, stop=True, skip_group_check=True), [tok["relout", s]], signal=blk == 1 and j == 3)
            tok["relsum", s] = mm

        def out_copy(s):
            tok["o_out", s] = ACTQ.do(lambda e: e.activation(oT[:].rearrange("p a q -> p (a q)"), oacc[:, 0:2 * P], ACT.Copy),
                                      [tok["pv_all", s], tok["relsum", s]] + get("o_tr", s - 1))

        def out_norm(s):
            n, t = divmod(s, T)
            b, g = divmod(n, G)
            i_, m, free = small_bank()
            for blk in range(2):
                tr = PE.do(lambda e, blk=blk, m=m: e.matmul(m[:, blk * P:(blk + 1) * P], oT[:, blk, :], ident[:],
                                                            start=True, stop=True, is_transpose=True),
                           [tok["o_out", s], free])
            tok["o_tr", s] = tr
            view = m[:, 0:2 * P].rearrange("p (h c) -> p h c", c=32)
            rc = DVE.do(lambda e: e.reciprocal(rsum[:], view[:, :, D]), [tr] + get("norm", s - 1))
            ev = DVE.do(lambda e: e.tensor_tensor(
                attn[:, t, g * P:(g + 1) * P].rearrange("p (h d) -> p h d", d=D), view[:, :, 0:D],
                rsum[:].rearrange("p (h o) -> p h o", o=1).broadcast_to([P, HG, D]), ALU.mult),
                [rc] + get("att_read", b - 1, t))
            freed(i_, ev)
            tok["norm", s] = ev

        xtile = a["x"].rearrange("(n p) h -> n p h", p=P)
        otile = out.rearrange("(n p) h -> n p h", p=P)
        last_tile = {}

        def tail_load(b, t):
            r = b * T + t
            tok["xt", r] = SP.dma(xt[r % 2][:], xtile[r], s_xt[r % 2], get("x1", r - 2))

        def transposed(src, dst, after, dst_free):
            i_, m, free = small_bank()
            for ih in range(2):
                tr = PE.do(lambda e, ih=ih, m=m: e.matmul(m[:, ih * P:(ih + 1) * P], src[:, ih * P:(ih + 1) * P], ident[:],
                                                          start=True, stop=True, is_transpose=True), after + [free])
            ev = ACTQ.do(lambda e, m=m: e.activation(dst[:].rearrange("p i t -> p (i t)"), m[:, 0:H], ACT.Copy),
                         [tr] + dst_free)
            freed(i_, ev)
            return tr, ev

        def linear(srcT, w, bias, dst, after, dst_free):
            i_, m, free = small_bank()
            for ih in range(2):
                mm = PE.do(lambda e, ih=ih, m=m: e.matmul(m[:, 0:H], srcT[:, ih, :], w[:, ih, :], start=ih == 0, stop=ih == 1),
                           after + [free], signal=ih == 1)
            ev = DVE.do(lambda e, m=m: e.tensor_tensor(dst[:], m[:, 0:H], bias[:], ALU.add), [mm] + dst_free)
            freed(i_, ev)
            return mm, ev

        def tail_attT(b, t):
            r = b * T + t
            tok["att_read", b, t], tok["attT", r] = transposed(attn[:, t, :], attT, [tok["norm", (b * G + 1) * T + t]],
                                                               get("wo", r - 1))

        def tail_wo(b, t):
            r = b * T + t
            y = ybuf[r % 2]
            tok["wo", r], ev = linear(attT, wo, bo, y, [tok["attT", r]], get("x1", r - 2))
            iv = inv_std(1, [y[:]], [ev])
            yn = normed(DVE, 1, 0, y[:], y[:], [iv])
            tok["x1", r] = POOL.do(lambda e: e.tensor_tensor(x1[r % 2][:], y[:], xt[r % 2][:], ALU.add),
                                   [yn, tok["xt", r]] + get("z", r - 2))

        def tail_norm(b, t):
            r = b * T + t
            iv = inv_std(2, [x1[r % 2][:]], [tok["x1", r]])
            tok["xn1", r] = normed(DVE, 2, 0, xn1[:], x1[r % 2][:], [iv] + get("x1tr", r - 1))

        def tail_x1T(b, t):
            r = b * T + t
            tok["x1tr", r], tok["x1T", r] = transposed(xn1, x1T, [tok["xn1", r]], get("ff", r - 1))

        def tail_ff(b, t):
            r = b * T + t
            z = zbuf[r % 2]
            tok["ff", r], ev = linear(x1T, wf, bf, z, [tok["x1T", r], wf_ready], get("stored", r - 2))
            iv = inv_std(1, [z[:]], [ev])
            zn = normed(DVE, 1, 0, z[:], z[:], [iv])
            tok["z", r] = POOL.do(lambda e: e.tensor_tensor(z[:], z[:], x1[r % 2][:], ALU.add), [zn])
            last_tile[r % 2] = tok["stored", r] = POOL.dma(otile[r], z[:], s_out[r % 2], [tok["z", r]])

        PE.wait([consts])
        ACTQ.wait([consts, vbase_ready])
        for c in range(NCHUNK):
            for stage in prep(0, c):
                stage()

        todo = {}

        def at(slot, f, *args):
            todo.setdefault(slot, []).append((f, args))

        for b in range(1, B):
            for c in range(NCHUNK):
                first = ((b - 1) * G * T + T + c) * HG + 12
                for x, stage in enumerate(prep(b, c)):
                    at(first + x, stage)
        for s in range(STEPS):
            n, t = divmod(s, T)
            b, g = divmod(n, G)
            z = s * HG
            if t == 0:
                at(z - 18, load_k, n)
            at(z - 24, load_q, s)
            for pair in range(HG // 2):
                at(z - 20 + pair, band_raw, s, pair)
            at(z - 16, band_write, s)
            at(z - 15, band_read, s)
            for h in range(HG):
                at(z - 12 + h, row_max, s, h)
            at(z - 5, max_reduce, s)
            at(z - 4, max_rows, s)
            for blk in range(2):
                o = z + 4 * blk
                for j in range(4):
                    at(o + j // 2, weights, s, 4 * blk + j, "X")
                at(o + 2, weights, s, 4 * blk, "Y")
                at(o + 2, weights, s, 4 * blk + 1, "Y")
                at(o + 3, weighted, s, blk, "X")
                at(o + 3, weights, s, 4 * blk + 2, "Y")
                at(o + 3, weights, s, 4 * blk + 3, "Y")
                at(o + 5, weighted, s, blk, "Y")
            at(z + 6, relative, s, 0)
            at(z + 7, relative, s, 1)
            at(z + 8, relative_sum, s)
            at(z + 9, out_copy, s)
            at(z + 10, out_norm, s)
            if g == 1:
                o = z + 11 if b == B - 1 else z + 11 + T * HG - HG
                at(o - 3, tail_load, b, t)
                at(o, tail_attT, b, t)
                at(o + 1, tail_wo, b, t)
                at(o + 4, tail_norm, b, t)
                at(o + 6, tail_x1T, b, t)
                at(o + 7, tail_ff, b, t)
        for slot in sorted(todo):
            for f, args in todo[slot]:
                f(*args)
        POOL.wait([last_tile[0], last_tile[1]])

        with nc.Block() as block:
            @block.sync
            def _(e):
                SP.run(e)

            @block.gpsimd
            def _(e):
                POOL.run(e)

            @block.tensor
            def _(e):
                PE.run(e)

            @block.vector
            def _(e):
                DVE.run(e)

            @block.scalar
            def _(e):
                ACTQ.run(e)


def kernel(L0_attn_x, L0_attn_mask, L0_attn_Wq, L0_attn_bq, L0_attn_Wk, L0_attn_bk, L0_attn_Wv, L0_attn_bv, L0_attn_Wo,
           L0_attn_bo, L0_attn_embK, L0_attn_embV, L0_ffn_weight, L0_ffn_alpha, L0_ffn_bias):
    from concourse import bacc
    from concourse.bass_utils import run_bass_kernel_spmd

    def arr(v):
        return np.asarray(v)

    order = np.arange(H).reshape(G, HG, D).transpose(0, 2, 1).reshape(-1)
    embK, embV = arr(L0_attn_embK), arr(L0_attn_embV)
    near = np.clip(np.arange(EXT) - EXT // 2, -MRP, MRP) + MRP
    p = np.arange(P)
    f32 = np.float32
    ins = {
        "x": arr(L0_attn_x).reshape(B * S, H),
        "WqT": arr(L0_attn_Wq).T[:, order], "WkT": arr(L0_attn_Wk).T[:, order],
        "WvT": arr(L0_attn_Wv).T, "WoT": arr(L0_attn_Wo).T, "WfT": arr(L0_ffn_weight).T,
        "bq": arr(L0_attn_bq)[order].reshape(G, P).T, "bk": arr(L0_attn_bk)[order].reshape(G, P).T,
        "bv": arr(L0_attn_bv), "bo": arr(L0_attn_bo), "bf": arr(L0_ffn_bias), "alpha": arr(L0_ffn_alpha),
        "efarV": np.stack([np.tile(embV[0], NH), np.tile(embV[-1], NH)]),
        "relbase": np.stack([embV[0], embV[-1]]),
        "extV": embV[near].reshape(-1),
        "kfar": np.stack([np.repeat(embK[0], HG), np.repeat(embK[-1], HG)], axis=1),
        "embk6": np.tile(embK.T, (NB, 1)),
        "ident": np.eye(P, dtype=f32),
        "headmask": (p[:, None] % HG == np.arange(HG)).astype(f32),
        "relmask": (QG - 1 - p[:, None] // D == np.arange(QG)).astype(f32),
        "relsum": (p[:, None] % D == np.arange(D)).astype(f32),
        "partmask": (np.repeat(KPARTS, D)[:, None] == np.arange(3)).astype(f32),
    }
    nc = bacc.Bacc("TRN2", target_bir_lowering=False, num_devices=1)
    aps = {}
    for k in ins:
        ins[k] = np.ascontiguousarray(ins[k])
        aps[k] = nc.dram_tensor("in_" + k, ins[k].shape, mybir.dt.from_np(ins[k].dtype), kind="ExternalInput").ap()
    out = nc.dram_tensor("out", (B * S, H), F32, kind="ExternalOutput").ap()
    build(nc, aps, out)
    r = run_bass_kernel_spmd(nc, [{"in_" + k: v for k, v in ins.items()}], core_ids=[0])
    return r.results[0]["out"].reshape(B, S, H)
```

```python
from contextlib import ExitStack

import numpy as np
import concourse.bass as bass
from concourse import mybir

F32 = mybir.dt.float32
BF16 = mybir.dt.bfloat16
I32 = mybir.dt.int32
ALU = mybir.AluOpType
ACT = mybir.ActivationFunctionType
AX = mybir.AxisListType

P = 128
B, S, H = 8, 1024, 256
NH, D, MRP = 16, 16, 64
VOCAB = 2 * MRP + 1
T = S // P
G = 2
HG = NH // G
STEPS = B * G * T
QPARTS = (0, 0, 0, 1, 1, 2)
KPARTS = (1, 0, 2, 0, 1, 0)
NB = len(QPARTS)
SPLIT = NB * D
FAR = SPLIT + 3
ROWS = FAR + 2
QDROWS = SPLIT + 6
CHUNK = 2
NCHUNK = T // CHUNK
CT = CHUNK * P
WIN = 2 * P
HALF = P // 2
FW, GW = P, HALF
PW = FW + GW
SLOT = WIN + HALF
VW = D + 1
QG = 8
NQG = P // QG
EXT = P + WIN - 1
EPS = 1e-5
LOWEST = -3.0e38
QRING, BRING, VRING = 4, 3, 3


class Sem:

    def __init__(self, handle):
        self.handle, self.value = handle, 0

    def up(self, n):
        self.value += n
        return (self, self.value)


class Queue:

    def __init__(self, done):
        self.items, self.done, self.seen = [], done, {}

    def wait(self, after):
        for sem, value in after:
            if self.seen.get(sem, 0) < value:
                self.seen[sem] = value
                self.items.append(lambda e, s=sem.handle, v=value: e.wait_ge(s, v))

    def do(self, f, after=(), signal=True):
        self.wait(after)
        if signal:
            tok = self.done.up(1)
            self.items.append(lambda e: f(e).then_inc(self.done.handle, 1))
            return tok
        self.items.append(f)
        return None

    def dma(self, out, in_, sem, after=()):
        self.wait(after)
        tok = sem.up(16)
        self.items.append(lambda e: e.dma_start(out, in_).then_inc(sem.handle, 16))
        return tok

    def run(self, engine):
        for f in self.items:
            f(engine)


def tile_layout(t):
    band = [k for k in (t - 1, t, t + 1) if 0 <= k < T]
    rest = [k for k in range(T) if k not in band]
    x = band + rest[:4 - len(band)]
    return x, rest[4 - len(band):]


def score_pieces(t):
    first = max(P * t - HALF, 0)
    runs = []
    for c in range(0, S, HALF):
        k = (c + first) % S
        side = "L" if k < P * t else "C" if k < P * t + P else "R"
        if runs and c % 512 and runs[-1][3] == side and runs[-1][1] + runs[-1][2] == k:
            runs[-1][2] += HALF
        else:
            runs.append([c, k, HALF, side])
    return runs


def window(t):
    width = WIN if 0 < t < T - 1 else WIN - HALF
    return width, HALF + (HALF if t == 0 else 0)


def build(nc, a, out):
    ctx = ExitStack()
    with ctx:
        def sb(name, shape, dt=F32):
            return ctx.enter_context(nc.sbuf_tensor(name, shape, dt))

        def ps(name, cols):
            return ctx.enter_context(nc.psum_tensor(name, [P, cols], F32))

        def sem(name):
            return Sem(ctx.enter_context(nc.semaphore(name)))

        scores = ps("scores", S)
        logitsT = [ps(f"logitsT{i}", 512) for i in range(3)]
        oacc = ps("oacc", 512)
        misc = [ps(f"misc{i}", 512) for i in range(2)]

        ident = sb("ident", [P, P])
        ones = sb("ones", [P, P])
        wq, wk, wv, wo, wf = (sb(n, [P, 2, H]) for n in ("wq", "wk", "wv", "wo", "wf"))
        bq, bk = sb("bq", [P, G]), sb("bk", [P, G])
        vbase = sb("vbase", [P, 2, H])
        bo, bf = sb("bo", [P, H]), sb("bf", [P, H])
        alpha = sb("alpha", [P, 1])
        relmask, relsum = sb("relmask", [P, QG]), sb("relsum", [P, D])
        headmask, kfar = sb("headmask", [P, HG]), sb("kfar", [P, 2])
        farw = sb("farw", [P, 2, HG])
        partmask = sb("partmask", [SPLIT, 3])
        embk6 = sb("embk6", [SPLIT, VOCAB])
        bandtab = [sb(f"bandtab{i}", [SPLIT, PW], BF16) for i in range(2)]
        reltab = sb("reltab", [P, WIN, D])
        relbase = sb("relbase", [P, 2, D])
        small = sb("small", [P, 8])

        ks = [sb(f"ks{i}", [ROWS, HG, S], BF16) for i in range(2)]
        qs = [sb(f"qs{i}", [ROWS, 2, HG, P], BF16) for i in range(QRING)]
        ql, qr = ([q_[:, side] for q_ in qs] for side in range(2))
        vl = [sb(f"vl{i}", [P, T, HG, VW]) for i in range(VRING)]
        vr = [sb(f"vr{i}", [P, T, HG, VW]) for i in range(VRING)]
        band = [sb(f"band{i}", [P, HG * SLOT + HALF]) for i in range(BRING)]
        praw = sb("praw", [P, HG, PW])
        wx = sb("wx", [P, HG, 512])
        wy = sb("wy", [P, 4, 512])
        junk = [sb(f"junk{i}", [P, WIN], BF16) for i in range(2)]
        maxes = [sb(f"maxes{i}", [P, HG, 3]) for i in range(2)]
        negmax = [sb(f"negmax{i}", [P, HG]) for i in range(2)]
        nm = sb("nm", [HG, 2, P], BF16)
        relout = sb("relout", [P, 2, 512])
        oT = sb("oT", [P, 2, P])
        rsum = sb("rsum", [P, HG])
        attn = sb("attn", [P, T, H])
        xc = sb("xc", [P, CHUNK, H])
        xnT = sb("xnT", [P, 2, CT])
        qf = sb("qf", [P, G, CT])
        qres = sb("qres", [P, G, CT])
        qp = [sb(f"qp{i}", [P, G, CT], BF16) for i in range(3)]
        fp = sb("fp", [2 * HG, 3, G, CT], BF16)
        attT, x1T = sb("attT", [P, 2, P]), sb("x1T", [P, 2, P])
        vb_raw = attT[:].rearrange("p i t -> p (i t)")
        xt = [sb(f"xt{i}", [P, H]) for i in range(2)]
        ybuf = [sb(f"ybuf{i}", [P, H]) for i in range(2)]
        x1 = [sb(f"x1_{i}", [P, H]) for i in range(2)]
        xn1 = sb("xn1", [P, H])
        zbuf = [sb(f"zbuf{i}", [P, H]) for i in range(2)]
        stats = [sb(f"stats{i}", [P, CHUNK, 6]) for i in range(4)]
        mv = [sb(f"mv{i}", [P, CHUNK, 2]) for i in range(4)]
        rs = [sb(f"rs{i}", [P, 4, CHUNK]) for i in range(4)]

        qd = [nc.dram_tensor(f"qd{i}", [G, QDROWS, HG, S], BF16).ap() for i in range(2)]
        kd = [nc.dram_tensor(f"kd{i}", [G, SPLIT, HG, S], BF16).ap() for i in range(2)]
        BROW = HALF + PW + P
        bs = [nc.dram_tensor(f"bs{i}", [HG, P, BROW], F32) for i in range(2)]
        nmd = [nc.dram_tensor(f"nmd{i}", [HG, 2, P], BF16) for i in range(2)]

        PE = Queue(sem("pe_done"))
        DVE = Queue(sem("dve_done"))
        ACTQ = Queue(sem("act_done"))
        POOL = Queue(sem("pool_done"))
        SP = Queue(sem("sp_done"))
        s_const, s_zero, s_x = sem("s_const"), sem("s_zero"), sem("s_x")
        s_chunk = {w: [[sem(f"s_{w}{i}_{c}") for c in range(NCHUNK)] for i in range(2)] for w in ("qd", "far", "kd")}
        s_ks = [[sem(f"s_ks{i}_{c}") for c in range(NCHUNK)] for i in range(2)]
        s_q = [sem(f"s_q{i}") for i in range(QRING)]
        s_nmw, s_nm = [sem(f"s_nmw{i}") for i in range(2)], [sem(f"s_nm{i}") for i in range(2)]
        s_bw, s_br = [sem(f"s_bw{i}") for i in range(2)], [sem(f"s_br{i}") for i in range(BRING)]
        s_xt, s_out = [sem(f"s_xt{i}") for i in range(2)], [sem(f"s_out{i}") for i in range(2)]

        def load(dst, src):
            return SP.dma(dst, src, s_const)

        for t_, n in ((wq, "WqT"), (wk, "WkT"), (wv, "WvT"), (wo, "WoT"), (wf, "WfT")):
            load(t_[:], a[n].rearrange("(i p) o -> p i o", p=P))
        for t_, n in ((ident, "ident"), (bq, "bq"), (bk, "bk"), (relmask, "relmask"), (relsum, "relsum"),
                      (headmask, "headmask"), (kfar, "kfar"), (partmask, "partmask"), (embk6, "embk6")):
            load(t_[:], a[n])
        for t_, n in ((vb_raw, "bv"), (bo[:], "bo"), (bf[:], "bf"), (alpha[:], "alpha")):
            load(t_, a[n].partition_broadcast(P))
        load(vbase[:], a["efarV"].partition_broadcast(P))
        load(relbase[:], a["relbase"].partition_broadcast(P))
        ext = a["extV"]
        consts = load(reltab[:].rearrange("p n d -> p (n d)"), bass.AP(ext.tensor, 0, [[D, P], [1, WIN * D]]))

        ones_set = POOL.do(lambda e: e.memset(ones[:], 1.0))
        cleared = []
        for t_ in band:
            cleared.append(POOL.do(lambda e, t_=t_: e.memset(t_[:], 0.0)))
        for i in range(2):
            zeroed = [SP.dma(bs[i].ap().rearrange("h p c -> p h c"),
                             band[0][:, 0:BROW].rearrange("p (h c) -> p h c", h=1).broadcast_to([P, HG, BROW]),
                             s_zero, [cleared[0]])]
        for t_ in vl + vr:
            DVE.do(lambda e, t_=t_: e.memset(t_[:, :, :, D:VW], 1.0))
        for t_ in ks:
            DVE.do(lambda e, t_=t_: e.memset(t_[SPLIT:ROWS, :, :], 1.0))
        v_ones = DVE.do(lambda e: e.memset(oacc[:], 0.0))
        reltab_ready = None
        for i, (n0, n1) in enumerate(((0, HALF + P), (HALF + P, WIN))):
            reltab_ready = POOL.do(lambda e, i=i, n0=n0, n1=n1: e.tensor_tensor(
                reltab[:, n0:n1, :], reltab[:, n0:n1, :],
                relbase[:, i:i + 1, :].broadcast_to([P, n1 - n0, D]), ALU.subtract), [consts])
        vbase_ready = None
        for i in range(2):
            vbase_ready = POOL.do(lambda e, i=i: e.tensor_tensor(vbase[:, i, :], vbase[:, i, :], vb_raw, ALU.add),
                                  [consts])
        for i in range(2):
            farw_ready = DVE.do(lambda e, i=i: e.tensor_scalar(farw[:, i, :], headmask[:], kfar[:, i:i + 1], None,
                                                               ALU.mult), [consts])
        bt_f, bt_p = ybuf[1], ybuf[0]
        jobs = [(0, 0, GW, 0, 0), (0, GW, FW, 0, VOCAB - 1), (1, 0, FW, 0, 0), (1, FW, GW, HALF, VOCAB - 1)]
        for tab, c, n, r, base in jobs:
            prev = DVE.do(lambda e, c=c, n=n, r=r, base=base: e.tensor_scalar(
                bt_f[0:SPLIT, c:c + n], embk6[:, r:r + n], embk6[:, base:base + 1], None, ALU.subtract),
                [consts, (DVE.done, DVE.done.value)])
            if c == 0:
                continue
            for part in range(3):
                prev = DVE.do(lambda e, tab=tab: e.tensor_copy(qp[0][0:SPLIT, 0, 0:PW], bt_f[0:SPLIT, 0:PW]), [prev])
                keep = bandtab[tab]
                if part == 0:
                    prev = DVE.do(lambda e, k=keep: e.tensor_scalar(
                        bt_p[0:SPLIT, 0:PW], qp[0][0:SPLIT, 0, 0:PW], partmask[:, 0:1], None, ALU.mult), [prev])
                else:
                    prev = DVE.do(lambda e, i=part: e.scalar_tensor_tensor(
                        bt_p[0:SPLIT, 0:PW], qp[0][0:SPLIT, 0, 0:PW], partmask[:, i:i + 1],
                        bt_p[0:SPLIT, 0:PW], ALU.mult, ALU.add), [prev])
                prev = DVE.do(lambda e: e.tensor_tensor(bt_f[0:SPLIT, 0:PW], bt_f[0:SPLIT, 0:PW],
                                                        qp[0][0:SPLIT, 0, 0:PW], ALU.subtract), [prev])
            tab_ready = DVE.do(lambda e, k=keep: e.tensor_copy(k[:, :], bt_p[0:SPLIT, 0:PW]), [prev])
        prev = DVE.do(lambda e: e.tensor_reduce(small[:, 0:1], wf[:], AX.XY, ALU.add, apply_absolute_value=True), [consts])
        prev = PE.do(lambda e: e.matmul(misc[0][:, 0:1], ones[:], small[:, 0:1], start=True, stop=True),
                     [prev, ones_set])
        prev = DVE.do(lambda e: e.tensor_scalar(small[:, 1:2], misc[0][:, 0:1], 1.0 / (H * H), 0.7, ALU.mult, ALU.mult), [prev])
        prev = DVE.do(lambda e: e.tensor_scalar(small[:, 2:3], small[:, 1:2], -1.0, None, ALU.mult), [prev])
        above, below = zbuf[0], zbuf[1]
        for i in range(2):
            DVE.do(lambda e, i=i: e.tensor_scalar(above[:], wf[:, i, :], small[:, 1:2], None, ALU.is_gt), [prev])
            prev = DVE.do(lambda e, i=i: e.tensor_scalar(below[:], wf[:, i, :], small[:, 2:3], None, ALU.is_lt), [prev])
            prev = DVE.do(lambda e, i=i: e.tensor_tensor(above[:], above[:], below[:], ALU.subtract), [prev])
            wf_ready = prev = DVE.do(lambda e, i=i: e.tensor_scalar(wf[:, i, :], above[:], alpha[:, 0:1], None, ALU.mult), [prev])

        bank = {"n": 0, "free": [wf_ready, v_ones]}

        def small_bank():
            i = bank["n"] % 2
            bank["n"] += 1
            return i, misc[i], bank["free"][i]

        def freed(i, tok):
            bank["free"][i] = tok

        ln_used = [[] for _ in range(4)]

        def inv_std(k, srcs, after):
            n = len(srcs)
            r = rs[k]
            for i, s_ in enumerate(srcs):
                prev = DVE.do(lambda e, s_=s_, i=i: e.bn_stats(stats[k][:, i, :], s_), after + ln_used[k])
            for i in range(n):
                prev = DVE.do(lambda e, i=i: e.bn_aggr(mv[k][:, i, :], stats[k][:, i, :]), [prev])
            prev = DVE.do(lambda e: e.tensor_scalar(r[:, 0, 0:n], mv[k][:, 0:n, 1], EPS, None, ALU.add), [prev])
            v, h_, y, w_ = (r[:, j, 0:n] for j in range(4))
            POOL.do(lambda e: e.tensor_scalar(h_, v, -0.5, None, ALU.mult), [prev])
            prev = POOL.do(lambda e: e.tensor_scalar(y.bitcast(I32), v.bitcast(I32), -0.5, float(0x5f3759df),
                                                     ALU.mult, ALU.add))
            for _ in range(3):
                prev = POOL.do(lambda e: e.tensor_tensor(w_, y, y, ALU.mult), [prev])
                prev = POOL.do(lambda e: e.tensor_tensor(w_, w_, h_, ALU.mult), [prev])
                prev = POOL.do(lambda e: e.tensor_scalar(w_, w_, 1.5, None, ALU.add), [prev])
                prev = POOL.do(lambda e: e.tensor_tensor(y, y, w_, ALU.mult), [prev])
            return prev

        def normed(q, k, i, dst, src, after):
            tok = q.do(lambda e: e.tensor_scalar(dst, src, mv[k][:, i, 0:1], rs[k][:, 2, i:i + 1],
                                                 ALU.subtract, ALU.mult), after)
            ln_used[k] = [tok]
            return tok

        xrow = a["x"].rearrange("(b c i p) h -> b c p i h", b=B, c=NCHUNK, i=CHUNK)
        st = {"xc": [], "xnT": [], "qf": [], "qp": [], "fp": [], "qres": []}
        q_loaded, k_loaded, v_written, v_read = {}, {}, {}, {}
        chunk_written = {}

        def prep(b, c):
            buf = b % 2
            loc = {}

            helper = DVE if b == 0 else POOL

            def load_x():
                loc["x"] = SP.dma(xc[:], xrow[b, c], s_x, st["xc"])

            def normalise():
                loc["rs"] = inv_std(0, [xc[:, i, :] for i in range(CHUNK)], [loc["x"]])

            def normalised():
                for i in range(CHUNK):
                    loc["xn"] = normed(helper, 0, i, xc[:, i, :], xc[:, i, :], [loc["rs"]])

            def transpose_x():
                i_, m, free = small_bank()
                for ih in range(2):
                    for i in range(CHUNK):
                        tr = PE.do(lambda e, ih=ih, i=i, m=m: e.matmul(
                            m[:, ih * CT + i * P:ih * CT + (i + 1) * P], xc[:, i, ih * P:(ih + 1) * P], ident[:],
                            start=True, stop=True, is_transpose=True), [loc["xn"], free, consts])
                st["xc"] = [tr]
                loc["xnT"] = ACTQ.do(lambda e, m=m: e.activation(xnT[:].rearrange("p i t -> p (i t)"), m[:, 0:2 * CT],
                                                                ACT.Copy), [tr] + st["xnT"])
                freed(i_, loc["xnT"])

            def project(w, bias):
                i_, m, free = small_bank()
                for g in range(G):
                    for ih in range(2):
                        mm = PE.do(lambda e, g=g, ih=ih, m=m: e.matmul(
                            m[:, g * CT:(g + 1) * CT], w[:, ih, g * P:(g + 1) * P], xnT[:, ih, :],
                            start=ih == 0, stop=ih == 1), [loc["xnT"], free], signal=ih == 1)
                for g in range(G):
                    for dst, used in ((qf, st["qf"]), (qp[0], st["qp"])):
                        ev = ACTQ.do(lambda e, g=g, m=m, dst=dst: e.activation(
                            dst[:, g, :], m[:, g * CT:(g + 1) * CT], ACT.Identity, bias=bias[:, g:g + 1]), [mm] + used)
                freed(i_, ev)
                prev = helper.do(lambda e: e.tensor_tensor(qres[:], qf[:], qp[0][:], ALU.subtract), [ev] + st["qres"])
                st["qf"] = [prev]
                prev = helper.do(lambda e: e.tensor_copy(qp[1][:], qres[:]), [prev] + st["qp"])
                prev = helper.do(lambda e: e.tensor_tensor(qp[2][:], qres[:], qp[1][:], ALU.subtract), [prev])
                st["qres"] = [prev]
                loc["split"] = prev
                return ev

            def write(parts, dram, rows, name):
                s_ = s_chunk[name][buf][c]
                for k in range(3):
                    at_ = [r for r in range(NB) if parts[r] == k]
                    step = at_[1] - at_[0] if len(at_) > 1 else 1
                    for g in range(G):
                        w_ = SP.dma(bass.AP(dram[buf].tensor, (g * rows + at_[0] * D) * HG * S + c * CT,
                                            [[S, P], [step * D * HG * S, len(at_)], [1, CT]]),
                                    qp[k][:, g:g + 1, :].broadcast_to([P, len(at_), CT]), s_,
                                    [loc["split"]] + chunk_reads(b - 2))
                st["qp"] = [w_]
                chunk_written.setdefault((b, c), []).append(w_)

            def project_q():
                loc["q"] = project(wq, bq)

            def write_q():
                write(QPARTS, qd, QDROWS, "qd")

            def far_rows():
                i_, m, free = small_bank()
                mm = PE.do(lambda e, m=m: e.matmul(m[0:2 * HG, 0:G * CT], farw[:].rearrange("p a h -> p (a h)"),
                                                   qf[:].rearrange("p g t -> p (g t)"), start=True, stop=True),
                           [loc["q"], farw_ready, free])
                st["qf"] = st["qf"] + [mm]
                fv = qres[0:2 * HG, :, :]
                mv_ = m[0:2 * HG, 0:G * CT].rearrange("p (g t) -> p g t", g=G)
                cp = DVE.do(lambda e: e.tensor_copy(fp[:, 0], mv_), [mm] + st["fp"])
                ev = DVE.do(lambda e: e.tensor_tensor(fv, mv_, fp[:, 0], ALU.subtract), [cp] + st["qres"])
                freed(i_, ev)
                cp = helper.do(lambda e: e.tensor_copy(fp[:, 1], fv), [ev])
                loc["far"] = helper.do(lambda e: e.tensor_tensor(fp[:, 2], fv, fp[:, 1], ALU.subtract), [cp])
                st["qres"] = [loc["far"]]

            def write_far():
                for g in range(G):
                    w_ = SP.dma(bass.AP(qd[buf].tensor, (g * QDROWS + SPLIT) * HG * S + c * CT,
                                        [[S, 2 * HG], [2 * HG * S, 3], [1, CT]]), fp[:, :, g, :],
                                s_chunk["far"][buf][c], [loc["far"]] + chunk_reads(b - 2))
                st["fp"] = [w_]
                chunk_written[b, c].append(w_)

            def project_k():
                project(wk, bk)

            def write_k():
                write(KPARTS, kd, SPLIT, "kd")

            def project_v():
                i_, m, free = small_bank()
                for i in range(CHUNK):
                    for ih in range(2):
                        mm = PE.do(lambda e, i=i, ih=ih, m=m: e.matmul(
                            m[:, i * H:(i + 1) * H], xnT[:, ih, i * P:(i + 1) * P], wv[:, ih, :],
                            start=ih == 0, stop=ih == 1), [loc["xnT"], free], signal=ih == 1)
                for side, ring in enumerate((vl, vr)):
                    for g in range(G):
                        n = b * G + g
                        ev = DVE.do(lambda e, side=side, ring=ring, g=g, n=n, m=m: e.tensor_tensor(
                            ring[n % VRING][:, c * CHUNK:(c + 1) * CHUNK, :, 0:D].rearrange("p i h d -> p i h d"),
                            m[:, 0:CHUNK * H].rearrange("p (i g h d) -> p g i h d", i=CHUNK, g=G, h=HG)[:, g],
                            vbase[:, side:side + 1, g * P:(g + 1) * P].rearrange("p a (h d) -> p a h d", h=HG)
                            .broadcast_to([P, CHUNK, HG, D]), ALU.add),
                            [mm, vbase_ready] + v_read.get(n - VRING, []))
                        v_written[n] = [ev]
                freed(i_, ev)

            def xnT_free():
                st["xnT"] = [(PE.done, PE.done.value)]

            return [(-7, load_x), (-5, normalise), (-2, normalised), (0, transpose_x), (1, project_q), (2, project_v),
                    (3, far_rows), (4, write_q), (4, project_k), (4, xnT_free), (5, write_far), (7, write_k)]

        def chunk_reads(b):
            if b < 0:
                return []
            return [q_loaded[s] for s in range(b * G * T, (b + 1) * G * T)][-QRING:] + \
                   [k_loaded[b * G + g, c] for g in range(G) for c in range(NCHUNK)]

        tok = {}

        def get(*key):
            return [tok[key]] if key in tok else []

        def load_k(n):
            b, g = divmod(n, G)
            for c in range(NCHUNK):
                k_loaded[n, c] = SP.dma(ks[n % 2][0:SPLIT, :, c * CT:(c + 1) * CT], kd[b % 2][g, :, :, c * CT:(c + 1) * CT],
                                        s_ks[n % 2][c], chunk_written[b, c] + [v_ones] + get("st_done", (n - 1) * T - 1))

        def load_q(s):
            n, t = divmod(s, T)
            b, g = divmod(n, G)
            i = s % QRING
            after = chunk_written[b, t // CHUNK] + get("st_done", s - QRING)
            src = qd[b % 2][g]
            for side in range(2):
                SP.dma(qs[i][0:SPLIT, side], src[0:SPLIT, :, t * P:(t + 1) * P], s_q[i], after)
                q_loaded[s] = SP.dma(qs[i][SPLIT:FAR, side],
                                     bass.AP(src.tensor, src.offset + (SPLIT + side) * HG * S + t * P,
                                             [[2 * HG * S, 3], [S, HG], [1, P]]), s_q[i], after)

        def band_raw(s, pair):
            i = s % QRING
            i_, m, free = small_bank()
            for j in range(2):
                h = 2 * pair + j
                for half in range(2):
                    mm = PE.do(lambda e, h=h, j=j, half=half, m=m: e.matmul(
                        m[HALF * half:HALF * (half + 1), j * PW:(j + 1) * PW],
                        ql[i][0:SPLIT, h, HALF * half:HALF * (half + 1)], bandtab[half][:], start=True, stop=True),
                        [q_loaded[s], tab_ready, free], signal=j == 1)
            ev = ACTQ.do(lambda e, m=m: e.activation(praw[:, 2 * pair:2 * pair + 2, :].rearrange("p h c -> p (h c)"),
                                                     m[:, 0:2 * PW], ACT.Copy), [mm] + get("bw", s - 1))
            freed(i_, ev)
            tok["praw", s] = ev

        def band_write(s):
            k = s % 2
            for half, c0 in ((0, HALF), (1, P)):
                rows = slice(HALF * half, HALF * (half + 1))
                tok["bw", s] = SP.dma(bs[k].ap()[:, rows, c0:c0 + PW].rearrange("h p c -> p h c"), praw[rows, :, :],
                                      s_bw[k], [tok["praw", s]] + zeroed + get("br", s - 2))

        def band_read(s):
            k, i = s % 2, s % BRING
            slots = band[i][:, 0:HG * SLOT].rearrange("p (h c) -> p h c", h=HG)
            after = [tok["bw", s], cleared[-1]] + get("st_done", s - BRING)
            for half, c0, o, w in ((0, HALF, HALF, HALF), (0, HALF + P, P, WIN - HALF),
                                   (1, HALF, HALF, WIN - HALF), (1, HALF + WIN, WIN, HALF)):
                rows = slice(HALF * half, HALF * (half + 1))
                tok["br", s] = SP.dma(slots[rows, :, o:o + w],
                                      bass.AP(bs[k], HALF * half * BROW + c0, [[BROW - 1, HALF], [P * BROW, HG], [1, w]]),
                                      s_br[i], after)

        def row_max(s, h):
            n, t = divmod(s, T)
            i, k, mx = s % QRING, ks[n % 2], maxes[s % 2]
            first = True
            kin = [k_loaded[n, c] for c in range(NCHUNK)] if t == 0 and h == 0 else []
            u = s * HG + h
            for c, key, length, side in score_pieces(t):
                after = [q_loaded[s]] + kin + get("max", u - 1, c // 512)
                last = c + length in (512, S)
                if side == "C":
                    for half, q_ in ((0, qr[i]), (1, ql[i])):
                        r = slice(HALF * half, HALF * (half + 1))
                        mm = PE.do(lambda e, r=r, q_=q_, c=c, key=key, length=length: e.matmul(
                            scores[r, c:c + length], q_[0:FAR, h, r], k[0:FAR, h, key:key + length],
                            start=True, stop=True), after, signal=last and half == 1)
                else:
                    q_ = ql[i] if side == "L" else qr[i]
                    mm = PE.do(lambda e, q_=q_, c=c, key=key, length=length: e.matmul(
                        scores[:, c:c + length], q_[0:FAR, h, :], k[0:FAR, h, key:key + length],
                        start=True, stop=True), after, signal=last)
                if c + length == 512:
                    full0 = mm
            width, off = window(t)
            bcol = h * SLOT + off
            mxfree = get("negmax", s - 2)
            DVE.do(lambda e: e.tensor_tensor_reduce(
                junk[u % 2][:, 0:width], scores[:, 0:width], band[s % BRING][:, bcol:bcol + width], 1.0, LOWEST,
                ALU.add, ALU.max, mx[:, h, 0:1]), [full0, tok["br", s]] + mxfree + get("max", u - 1, 1) + [tab_ready])
            tok["max", u, 0] = DVE.do(lambda e: e.tensor_reduce(mx[:, h, 1:2], scores[:, width:512], AX.X, ALU.max))
            tok["max", u, 1] = DVE.do(lambda e: e.tensor_reduce(mx[:, h, 2:3], scores[:, 512:S], AX.X, ALU.max), [mm])

        def max_reduce(s):
            tok["negmax", s] = DVE.do(lambda e: e.tensor_reduce(negmax[s % 2][:], maxes[s % 2][:], AX.X, ALU.max, negate=True),
                                      [tok["max", s * HG + HG - 1, 1]] + get("nmT", s - 2))

        def max_rows(s):
            i_, m, free = small_bank()
            tr = PE.do(lambda e, m=m: e.matmul(m[0:HG, 0:P], negmax[s % 2][:], ident[:], start=True, stop=True,
                                               is_transpose=True), [tok["negmax", s], free])
            tok["nmT", s] = tr
            c1 = DVE.do(lambda e, m=m: e.tensor_copy(nm[:, 0], m[0:HG, 0:P]), [tr] + get("nmw", s - 1))
            tok["nm2", s] = DVE.do(lambda e, m=m: e.tensor_tensor(nm[:, 1], m[0:HG, 0:P], nm[:, 0], ALU.subtract), [c1])
            freed(i_, tok["nm2", s])

        def max_write(s):
            tok["nmw", s] = SP.dma(nmd[s % 2].ap(), nm[:], s_nmw[s % 2], [tok["nm2", s]] + get("nm", s - 2))

        def max_read(s):
            for side in range(2):
                tok["nm", s] = SP.dma(qs[s % QRING][FAR:ROWS, side],
                                      bass.AP(nmd[s % 2], 0, [[P, 2], [2 * P, HG], [1, P]]), s_nm[s % 2],
                                      [tok["nmw", s]] + get("st_done", s - QRING))

        bankT = {"n": 0}
        exp_tok = {}

        def weights(s, h, kind):
            n, t = divmod(s, T)
            i, k = s % QRING, ks[n % 2]
            tiles = tile_layout(t)[0 if kind == "X" else 1]
            j = bankT["n"] % 3
            bankT["n"] += 1
            m = logitsT[j]
            after = [tok["nm", s], q_loaded[s]] + get("exp", bankT["n"] - 4)
            for c, kt in enumerate(tiles):
                lhs = k[0:ROWS, h, kt * P:(kt + 1) * P]
                band_tile = kind == "X" and abs(kt - t) <= 1
                last = c == len(tiles) - 1
                if kt == t:
                    for half, q_ in ((0, qr[i]), (1, ql[i])):
                        mm = PE.do(lambda e, c=c, half=half, q_=q_, lhs=lhs: e.matmul(
                            m[:, c * P + HALF * half:c * P + HALF * (half + 1)], lhs,
                            q_[0:ROWS, h, HALF * half:HALF * (half + 1)], start=half == 0, stop=not band_tile,
                            skip_group_check=True), after, signal=False)
                else:
                    q_ = ql[i] if kt < t else qr[i]
                    mm = PE.do(lambda e, c=c, q_=q_, lhs=lhs: e.matmul(
                        m[:, c * P:(c + 1) * P], lhs, q_[0:ROWS, h, :], start=True, stop=not band_tile,
                        skip_group_check=True), after, signal=last and not band_tile)
                if band_tile:
                    bc = h * SLOT + (kt - t + 1) * P
                    mm = PE.do(lambda e, c=c, bc=bc: e.matmul(
                        m[:, c * P:(c + 1) * P], band[s % BRING][:, bc:bc + P], ident[:], start=False, stop=True,
                        is_transpose=True, skip_group_check=True), [tok["br", s]], signal=last)
            tok["st_done", s] = mm
            if kind == "X":
                dst, free = wx[:, h, :], get("rel", s - 1) + get("pvX", s - 1, h // 4)
            else:
                dst = wy[:, h % 4, :]
                free = get("pvY", s - 1, 1) if h < 4 else get("pvY", s, 0)
            e_ = ACTQ.do(lambda e: e.activation(dst, m[:], ACT.Exp), [mm] + free)
            tok["exp", bankT["n"] - 1] = e_
            exp_tok[s, h, kind] = e_

        def weighted(s, blk, kind):
            n, t = divmod(s, T)
            tiles = tile_layout(t)[0 if kind == "X" else 1]
            VL, VR = vl[n % VRING], vr[n % VRING]
            after = [exp_tok[s, 4 * blk + j, kind] for j in range(4)] + v_written[n]
            if blk == 0 and kind == "X":
                after = after + get("o_out", s - 1)
            for c, kt in enumerate(tiles):
                for j in range(4):
                    h = 4 * blk + j
                    V = VL if kt <= t else VR
                    src = wx[:, h, :] if kind == "X" else wy[:, j, :]
                    mm = PE.do(lambda e, V=V, h=h, j=j, c=c, kt=kt, src=src: e.matmul(
                        oacc[32 * j:32 * j + VW, blk * P:(blk + 1) * P], V[:, kt, h, :], src[:, c * P:(c + 1) * P],
                        start=blk == 0 and kind == "X" and c == 0, stop=True, skip_group_check=True),
                        after, signal=c == len(tiles) - 1 and j == 3)
            tok["pv" + kind, s, blk] = mm
            if kind == "Y" and blk == 1:
                v_read[n] = [mm]
                tok["pv_all", s] = mm

        def relative(s, part):
            t = s % T
            tiles = tile_layout(t)[0]
            i_, m, free = small_bank()
            after = [exp_tok[s, h, "X"] for h in range(HG)] + [free, reltab_ready]
            for gq in range(NQG // 2):
                q0 = (part * NQG // 2 + gq) * QG
                near = [kt for kt in ((t - 1, t) if q0 < HALF else (t, t + 1)) if 0 <= kt < T]
                for x, kt in enumerate(near):
                    n0 = P * (kt - t) - (q0 + QG - 1) + (EXT // 2)
                    c = tiles.index(kt) * P + q0
                    mm = PE.do(lambda e, n0=n0, c=c, gq=gq, x=x, m=m, near=near: e.matmul(
                        m[:, gq * HG * QG:(gq + 1) * HG * QG], reltab[:, n0:n0 + QG, :].rearrange("p n d -> p (n d)"),
                        wx[:, :, c:c + QG], start=x == 0, stop=x == len(near) - 1),
                        after, signal=gq == NQG // 2 - 1 and x == len(near) - 1)
            if part == 1:
                tok["rel", s] = mm
            ev = DVE.do(lambda e, m=m: e.tensor_tensor(
                relout[:, part, :].rearrange("p (a c) -> p a c", c=QG), m[:].rearrange("p (a c) -> p a c", c=QG),
                relmask[:].rearrange("p (a c) -> p a c", a=1).broadcast_to([P, 512 // QG, QG]), ALU.mult),
                [mm] + get("relsum", s - 1))
            freed(i_, ev)
            tok["relout", s] = ev

        def relative_sum(s):
            src = relout[:].rearrange("p a (g h c) -> p (a g) h c", h=HG, c=QG)
            for blk in range(2):
                for j in range(4):
                    h = 4 * blk + j
                    mm = PE.do(lambda e, h=h, j=j, blk=blk: e.matmul(
                        oacc[32 * j:32 * j + D, blk * P:(blk + 1) * P], relsum[:], src[:, :, h, :],
                        start=False, stop=True, skip_group_check=True), [tok["relout", s]], signal=blk == 1 and j == 3)
            tok["relsum", s] = mm

        def out_copy(s):
            tok["o_out", s] = ACTQ.do(lambda e: e.activation(oT[:].rearrange("p a q -> p (a q)"), oacc[:, 0:2 * P], ACT.Copy),
                                      [tok["pv_all", s], tok["relsum", s]] + get("o_tr", s - 1))

        def out_norm(s):
            n, t = divmod(s, T)
            b, g = divmod(n, G)
            i_, m, free = small_bank()
            for blk in range(2):
                tr = PE.do(lambda e, blk=blk, m=m: e.matmul(m[:, blk * P:(blk + 1) * P], oT[:, blk, :], ident[:],
                                                            start=True, stop=True, is_transpose=True),
                           [tok["o_out", s], free])
            tok["o_tr", s] = tr
            view = m[:, 0:2 * P].rearrange("p (h c) -> p h c", c=32)
            rc = DVE.do(lambda e: e.reciprocal(rsum[:], view[:, :, D]), [tr] + get("norm", s - 1))
            ev = DVE.do(lambda e: e.tensor_tensor(
                attn[:, t, g * P:(g + 1) * P].rearrange("p (h d) -> p h d", d=D), view[:, :, 0:D],
                rsum[:].rearrange("p (h o) -> p h o", o=1).broadcast_to([P, HG, D]), ALU.mult),
                [rc] + get("att_read", b - 1, t))
            freed(i_, ev)
            tok["norm", s] = ev

        xtile = a["x"].rearrange("(n p) h -> n p h", p=P)
        otile = out.rearrange("(n p) h -> n p h", p=P)
        last_tile = {}

        def tail_load(b, t):
            r = b * T + t
            tok["xt", r] = SP.dma(xt[r % 2][:], xtile[r], s_xt[r % 2], get("x1", r - 2))

        def transposed(src, dst, after, dst_free):
            i_, m, free = small_bank()
            for ih in range(2):
                tr = PE.do(lambda e, ih=ih, m=m: e.matmul(m[:, ih * P:(ih + 1) * P], src[:, ih * P:(ih + 1) * P], ident[:],
                                                          start=True, stop=True, is_transpose=True), after + [free])
            ev = ACTQ.do(lambda e, m=m: e.activation(dst[:].rearrange("p i t -> p (i t)"), m[:, 0:H], ACT.Copy),
                         [tr] + dst_free)
            freed(i_, ev)
            return tr, ev

        def linear(srcT, w, bias, dst, after, dst_free):
            i_, m, free = small_bank()
            for ih in range(2):
                mm = PE.do(lambda e, ih=ih, m=m: e.matmul(m[:, 0:H], srcT[:, ih, :], w[:, ih, :], start=ih == 0, stop=ih == 1),
                           after + [free], signal=ih == 1)
            ev = DVE.do(lambda e, m=m: e.tensor_tensor(dst[:], m[:, 0:H], bias[:], ALU.add), [mm] + dst_free)
            freed(i_, ev)
            return mm, ev

        def tail_attT(b, t):
            r = b * T + t
            tok["att_read", b, t], tok["attT", r] = transposed(attn[:, t, :], attT, [tok["norm", (b * G + 1) * T + t]],
                                                               get("wo", r - 1))

        def tail_wo(b, t):
            r = b * T + t
            y = ybuf[r % 2]
            tok["wo", r], ev = linear(attT, wo, bo, y, [tok["attT", r]], get("x1", r - 2))
            tok["iy", r] = inv_std(1, [y[:]], [ev])

        def tail_x1(b, t):
            r = b * T + t
            y = ybuf[r % 2]
            yn = normed(DVE, 1, 0, y[:], y[:], [tok["iy", r]])
            tok["x1", r] = POOL.do(lambda e: e.tensor_tensor(x1[r % 2][:], y[:], xt[r % 2][:], ALU.add),
                                   [yn, tok["xt", r]] + get("z", r - 2))

        def tail_norm(b, t):
            r = b * T + t
            tok["ix", r] = inv_std(2, [x1[r % 2][:]], [tok["x1", r]])

        def tail_normed(b, t):
            r = b * T + t
            iv = tok["ix", r]
            tok["xn1", r] = normed(DVE, 2, 0, xn1[:], x1[r % 2][:], [iv] + get("x1tr", r - 1))

        def tail_x1T(b, t):
            r = b * T + t
            tok["x1tr", r], tok["x1T", r] = transposed(xn1, x1T, [tok["xn1", r]], get("ff", r - 1))

        def tail_ff(b, t):
            r = b * T + t
            z = zbuf[r % 2]
            tok["ff", r], ev = linear(x1T, wf, bf, z, [tok["x1T", r], wf_ready], get("stored", r - 2))
            tok["iz", r] = inv_std(3, [z[:]], [ev])

        def tail_out(b, t):
            r = b * T + t
            z = zbuf[r % 2]
            zn = normed(DVE, 3, 0, z[:], z[:], [tok["iz", r]])
            tok["z", r] = POOL.do(lambda e: e.tensor_tensor(z[:], z[:], x1[r % 2][:], ALU.add), [zn])

        def tail_store(b, t):
            r = b * T + t
            last_tile[r % 2] = tok["stored", r] = SP.dma(otile[r], zbuf[r % 2][:], s_out[r % 2], [tok["z", r]])

        PE.wait([consts])
        ACTQ.wait([consts, vbase_ready])
        todo = {}

        def at(slot, f, *args):
            todo.setdefault(slot, []).append((f, args))

        for b in range(B):
            for c in range(NCHUNK):
                first = ((b - 1) * G * T + T + c) * HG + 12 if b else 8 * c - 60
                for x, stage in prep(b, c):
                    at(first + x, stage)
        for s in range(STEPS):
            n, t = divmod(s, T)
            b, g = divmod(n, G)
            z = s * HG
            if t == 0:
                at(z - 18, load_k, n)
            at(z - 24, load_q, s)
            for pair in range(HG // 2):
                at(z - 20 + pair, band_raw, s, pair)
            at(z - 16, band_write, s)
            at(z - 15, band_read, s)
            for h in range(HG):
                at(z - 12 + h, row_max, s, h)
            at(z - 5, max_reduce, s)
            at(z - 4, max_rows, s)
            at(z - 3, max_write, s)
            at(z - 2, max_read, s)
            for blk in range(2):
                o = z + 4 * blk
                for j in range(4):
                    at(o + j // 2, weights, s, 4 * blk + j, "X")
                at(o + 2, weights, s, 4 * blk, "Y")
                at(o + 2, weights, s, 4 * blk + 1, "Y")
                at(o + 3, weighted, s, blk, "X")
                at(o + 3, weights, s, 4 * blk + 2, "Y")
                at(o + 3, weights, s, 4 * blk + 3, "Y")
                at(o + 5, weighted, s, blk, "Y")
            at(z + 6, relative, s, 0)
            at(z + 7, relative, s, 1)
            at(z + 8, relative_sum, s)
            at(z + 9, out_copy, s)
            at(z + 10, out_norm, s)
            if g == 1:
                o = z + 11 if b == B - 1 else z + 11 + T * HG - HG
                for x, f in enumerate((tail_load, None, None, tail_attT, tail_wo, None, tail_x1, tail_norm, None, tail_normed,
                                       tail_x1T, tail_ff, None, tail_out, tail_store)):
                    if f:
                        at(o - 3 + x, f, b, t)
        for slot in sorted(todo):
            for f, args in todo[slot]:
                f(*args)
        SP.wait([last_tile[0], last_tile[1]])

        with nc.Block() as block:
            @block.sync
            def _(e):
                SP.run(e)

            @block.gpsimd
            def _(e):
                POOL.run(e)

            @block.tensor
            def _(e):
                PE.run(e)

            @block.vector
            def _(e):
                DVE.run(e)

            @block.scalar
            def _(e):
                ACTQ.run(e)


def kernel(L0_attn_x, L0_attn_mask, L0_attn_Wq, L0_attn_bq, L0_attn_Wk, L0_attn_bk, L0_attn_Wv, L0_attn_bv, L0_attn_Wo,
           L0_attn_bo, L0_attn_embK, L0_attn_embV, L0_ffn_weight, L0_ffn_alpha, L0_ffn_bias):
    from concourse import bacc
    from concourse.bass_utils import run_bass_kernel_spmd

    def arr(v):
        return np.asarray(v)

    order = np.arange(H).reshape(G, HG, D).transpose(0, 2, 1).reshape(-1)
    embK, embV = arr(L0_attn_embK), arr(L0_attn_embV)
    near = np.clip(np.arange(EXT) - EXT // 2, -MRP, MRP) + MRP
    p = np.arange(P)
    f32 = np.float32
    ins = {
        "x": arr(L0_attn_x).reshape(B * S, H),
        "WqT": arr(L0_attn_Wq).T[:, order], "WkT": arr(L0_attn_Wk).T[:, order],
        "WvT": arr(L0_attn_Wv).T, "WoT": arr(L0_attn_Wo).T, "WfT": arr(L0_ffn_weight).T,
        "bq": arr(L0_attn_bq)[order].reshape(G, P).T, "bk": arr(L0_attn_bk)[order].reshape(G, P).T,
        "bv": arr(L0_attn_bv), "bo": arr(L0_attn_bo), "bf": arr(L0_ffn_bias), "alpha": arr(L0_ffn_alpha),
        "efarV": np.stack([np.tile(embV[0], NH), np.tile(embV[-1], NH)]),
        "relbase": np.stack([embV[0], embV[-1]]),
        "extV": embV[near].reshape(-1),
        "kfar": np.stack([np.repeat(embK[0], HG), np.repeat(embK[-1], HG)], axis=1),
        "embk6": np.tile(embK.T, (NB, 1)),
        "ident": np.eye(P, dtype=f32),
        "headmask": (p[:, None] % HG == np.arange(HG)).astype(f32),
        "relmask": (QG - 1 - p[:, None] // D == np.arange(QG)).astype(f32),
        "relsum": (p[:, None] % D == np.arange(D)).astype(f32),
        "partmask": (np.repeat(KPARTS, D)[:, None] == np.arange(3)).astype(f32),
    }
    nc = bacc.Bacc("TRN2", target_bir_lowering=False, num_devices=1)
    aps = {}
    for k in ins:
        ins[k] = np.ascontiguousarray(ins[k])
        aps[k] = nc.dram_tensor("in_" + k, ins[k].shape, mybir.dt.from_np(ins[k].dtype), kind="ExternalInput").ap()
    out = nc.dram_tensor("out", (B * S, H), F32, kind="ExternalOutput").ap()
    build(nc, aps, out)
    r = run_bass_kernel_spmd(nc, [{"in_" + k: v for k, v in ins.items()}], core_ids=[0])
    return r.results[0]["out"].reshape(B, S, H)
```

```python
from contextlib import ExitStack

import numpy as np
import concourse.bass as bass
from concourse import mybir

F32 = mybir.dt.float32
BF16 = mybir.dt.bfloat16
I32 = mybir.dt.int32
ALU = mybir.AluOpType
ACT = mybir.ActivationFunctionType
AX = mybir.AxisListType

P = 128
B, S, H = 8, 1024, 256
NH, D, MRP = 16, 16, 64
VOCAB = 2 * MRP + 1
T = S // P
G = 2
HG = NH // G
STEPS = B * G * T
QPARTS = (0, 0, 0, 1, 1, 2)
KPARTS = (1, 0, 2, 0, 1, 0)
NB = len(QPARTS)
SPLIT = NB * D
FAR = SPLIT + 3
ROWS = FAR + 2
QDROWS = SPLIT + 6
CHUNK = 2
NCHUNK = T // CHUNK
CT = CHUNK * P
WIN = 2 * P
HALF = P // 2
FW, GW = P, HALF
PW = FW + GW
VW = D + 1
QG = 8
NQG = P // QG
NEAR = 3 * P
EXT = P + WIN - 1
EPS = 1e-5
LOWEST = -3.0e38
QRING, BRING, VRING = 4, 3, 3


class Sem:

    def __init__(self, handle):
        self.handle, self.value = handle, 0

    def up(self, n):
        self.value += n
        return (self, self.value)


class Queue:

    def __init__(self, done):
        self.items, self.done, self.seen = [], done, {}

    def wait(self, after):
        for sem, value in after:
            if self.seen.get(sem, 0) < value:
                self.seen[sem] = value
                self.items.append(lambda e, s=sem.handle, v=value: e.wait_ge(s, v))

    def do(self, f, after=(), signal=True):
        self.wait(after)
        if signal:
            tok = self.done.up(1)
            self.items.append(lambda e: f(e).then_inc(self.done.handle, 1))
            return tok
        self.items.append(f)
        return None

    def dma(self, out, in_, sem, after=()):
        self.wait(after)
        tok = sem.up(16)
        self.items.append(lambda e: e.dma_start(out, in_).then_inc(sem.handle, 16))
        return tok

    def run(self, engine):
        for f in self.items:
            f(engine)


def tile_layout(t):
    rest = [k for k in range(T) if abs(k - t) > 1]
    x = [k if 0 <= k < T else rest.pop(0) for k in (t - 1, t, t + 1)] + [rest.pop(0)]
    return x, rest


def score_pieces(t):
    first = max(P * t - HALF, 0)
    runs = []
    for c in range(0, S, HALF):
        k = (c + first) % S
        side = "L" if k < P * t else "C" if k < P * t + P else "R"
        if runs and c % 512 and runs[-1][3] == side and runs[-1][1] + runs[-1][2] == k:
            runs[-1][2] += HALF
        else:
            runs.append([c, k, HALF, side])
    return runs


def window(t):
    width = WIN if 0 < t < T - 1 else WIN - HALF
    return width, HALF if t == 0 else 0


def build(nc, a, out):
    ctx = ExitStack()
    with ctx:
        def sb(name, shape, dt=F32):
            return ctx.enter_context(nc.sbuf_tensor(name, shape, dt))

        def ps(name, cols):
            return ctx.enter_context(nc.psum_tensor(name, [P, cols], F32))

        def sem(name):
            return Sem(ctx.enter_context(nc.semaphore(name)))

        scores = ps("scores", S)
        logitsT = [ps(f"logitsT{i}", 512) for i in range(3)]
        oacc = ps("oacc", 512)
        misc = [ps(f"misc{i}", 512) for i in range(2)]

        ident = sb("ident", [P, P])
        wq, wk, wv, wo, wf = (sb(n, [P, 2, H]) for n in ("wq", "wk", "wv", "wo", "wf"))
        bq, bk = sb("bq", [P, G]), sb("bk", [P, G])
        vbase = sb("vbase", [P, 2, H])
        bo, bf = sb("bo", [P, H]), sb("bf", [P, H])
        alpha = sb("alpha", [P, 1])
        relmask, relsum = sb("relmask", [P, QG]), sb("relsum", [P, D])
        headmask, kfar = sb("headmask", [P, HG]), sb("kfar", [P, 2])
        farw = sb("farw", [P, 2, HG])
        partmask = sb("partmask", [SPLIT, 3])
        embk6 = sb("embk6", [SPLIT, VOCAB])
        bandtab = [sb(f"bandtab{i}", [SPLIT, PW], BF16) for i in range(2)]
        reltab = sb("reltab", [P, WIN, D])
        relbase = sb("relbase", [P, 2, D])
        small = sb("small", [P, 8])

        ks = [sb(f"ks{i}", [ROWS, HG, S], BF16) for i in range(2)]
        qs = [sb(f"qs{i}", [ROWS, 2, HG, P], BF16) for i in range(QRING)]
        ql, qr = ([q_[:, side] for q_ in qs] for side in range(2))
        vl = [sb(f"vl{i}", [P, T, HG, VW]) for i in range(VRING)]
        vr = [sb(f"vr{i}", [P, T, HG, VW]) for i in range(VRING)]
        band = [sb(f"band{i}", [P, HG, WIN]) for i in range(BRING)]
        praw = sb("praw", [P, HG, PW])
        wx = sb("wx", [P, 2, HG, NEAR])
        wr = sb("wr", [P, 4, P])
        wy = sb("wy", [P, 4, 512])
        junk = sb("junk", [P, WIN], BF16)
        maxes = [sb(f"maxes{i}", [P, HG, 3]) for i in range(2)]
        negmax = [sb(f"negmax{i}", [P, HG]) for i in range(2)]
        nm = sb("nm", [HG, 2, P], BF16)
        relout = sb("relout", [P, 2, 512])
        oT = sb("oT", [P, 2, 2, P])
        rsum = sb("rsum", [P, HG])
        attn = sb("attn", [P, T, H])
        xc = sb("xc", [P, CHUNK, H])
        xnT = sb("xnT", [P, 2, CT])
        qf = sb("qf", [P, G, CT])
        qres = sb("qres", [P, G, CT])
        qparts, kparts = (sb(n, [P, 3, G, CT], BF16) for n in ("qparts", "kparts"))
        fparts = kparts[0:2 * HG]
        rowsT = sb("rowsT", [P, 2, P])
        vb_raw = rowsT[:].rearrange("p i t -> p (i t)")
        ybuf = sb("ybuf", [P, H])
        x1 = [sb(f"x1_{i}", [P, H]) for i in range(2)]
        zbuf = [sb(f"zbuf{i}", [P, H]) for i in range(2)]
        stats = [sb(f"stats{i}", [P, CHUNK, 6]) for i in range(4)]
        mv = [sb(f"mv{i}", [P, CHUNK, 2]) for i in range(4)]
        rs = [sb(f"rs{i}", [P, 4, CHUNK]) for i in range(4)]

        qd = [nc.dram_tensor(f"qd{i}", [G, QDROWS, HG, S], BF16).ap() for i in range(2)]
        kd = [nc.dram_tensor(f"kd{i}", [G, SPLIT, HG, S], BF16).ap() for i in range(2)]
        BROW = HALF + PW + P
        bs = [nc.dram_tensor(f"bs{i}", [HG, P, BROW], F32) for i in range(2)]
        nmd = [nc.dram_tensor(f"nmd{i}", [2, HG, P], BF16) for i in range(2)]

        PE = Queue(sem("pe_done"))
        DVE = Queue(sem("dve_done"))
        ACTQ = Queue(sem("act_done"))
        POOL = Queue(sem("pool_done"))
        SP = Queue(sem("sp_done"))
        s_const, s_table, s_zero, s_x = sem("s_const"), sem("s_table"), sem("s_zero"), sem("s_x")
        s_ident, s_reltab = sem("s_ident"), sem("s_reltab")
        s_x0 = [sem(f"s_x0_{c}") for c in range(NCHUNK)]
        s_chunk = {w: [[sem(f"s_{w}{i}_{c}") for c in range(NCHUNK)] for i in range(2)] for w in ("qd", "far", "kd")}
        s_ks = [[sem(f"s_ks{i}_{c}") for c in range(NCHUNK)] for i in range(2)]
        s_q = [sem(f"s_q{i}") for i in range(QRING)]
        s_nmw, s_nm = [sem(f"s_nmw{i}") for i in range(2)], [sem(f"s_nm{i}") for i in range(2)]
        s_bw, s_br = [sem(f"s_bw{i}") for i in range(2)], [sem(f"s_br{i}") for i in range(BRING)]
        s_xt, s_out = [sem(f"s_xt{i}") for i in range(2)], [sem(f"s_out{i}") for i in range(2)]

        cleared = POOL.do(lambda e: e.memset(band[0][:, 0:2, :], 0.0))
        xrow = a["x"].rearrange("(b c i p) h -> b c p i h", b=B, c=NCHUNK, i=CHUNK)
        x0_loaded = [SP.dma(attn[:, 0:CHUNK, :], xrow[0, 0], s_x0[0])]
        ident_loaded = SP.dma(ident[:], a["ident"], s_ident)
        for t_, n in ((wq, "WqT"), (wk, "WkT"), (wv, "WvT"), (bq, "bq"), (bk, "bk"),
                      (headmask, "headmask"), (kfar, "kfar")):
            src = a[n].rearrange("(i p) o -> p i o", p=P) if n.startswith("W") else a[n]
            SP.dma(t_[:], src, s_const)
        SP.dma(vb_raw, a["bv"].partition_broadcast(P), s_const)
        consts = SP.dma(vbase[:], a["efarV"].partition_broadcast(P), s_const)
        for c in range(1, NCHUNK):
            x0_loaded.append(SP.dma(attn[:, c * CHUNK:(c + 1) * CHUNK, :], xrow[0, c], s_x0[c]))
        for t_, n in ((wf, "WfT"), (wo, "WoT"), (relmask, "relmask"), (relsum, "relsum"), (partmask, "partmask"),
                      (embk6, "embk6")):
            src = a[n].rearrange("(i p) o -> p i o", p=P) if n.startswith("W") else a[n]
            tables = SP.dma(t_[:], src, s_table)
        for t_, n in ((bo, "bo"), (bf, "bf"), (alpha, "alpha"), (relbase, "relbase")):
            tables = SP.dma(t_[:], a[n].partition_broadcast(P), s_table)
        for i in range(2):
            zeroed = [SP.dma(bs[i].ap().rearrange("h p c -> p h c"),
                             band[0][:].rearrange("p h c -> p (h c)")[:, 0:BROW].rearrange("p (h c) -> p h c", h=1)
                             .broadcast_to([P, HG, BROW]), s_zero, [cleared])]
        ext = a["extV"]
        reltab_loaded = SP.dma(reltab[:].rearrange("p n d -> p (n d)"), bass.AP(ext.tensor, 0, [[D, P], [1, WIN * D]]), s_reltab)
        ones = ybuf[:, 0:P]
        ones_set = POOL.do(lambda e: e.memset(ones, 1.0))
        cleared = []
        oacc_zero = DVE.do(lambda e: e.memset(oacc[:], 0.0))
        vbase_ready = None
        for i in range(2):
            vbase_ready = POOL.do(lambda e, i=i: e.tensor_tensor(vbase[:, i, :], vbase[:, i, :], vb_raw, ALU.add),
                                  [consts])
        for i in range(2):
            farw_ready = DVE.do(lambda e, i=i: e.tensor_scalar(farw[:, i, :], headmask[:], kfar[:, i:i + 1], None,
                                                               ALU.mult), [consts])
        bank = {"n": 0, "held": None, "free": [oacc_zero, oacc_zero]}

        def small_bank():
            i = bank["n"] % 2
            if i == bank["held"]:
                i = 1 - i
            bank["n"] = i + 1
            return i, misc[i], bank["free"][i]

        def freed(i, tok):
            bank["free"][i] = tok

        tok = {}
        used = {"rowsT": [vbase_ready], "y": []}

        def set_k_ones(i):
            tok["k_ones", i] = POOL.do(lambda e: e.memset(ks[i][SPLIT:ROWS, :, :], 1.0), [(POOL.done, POOL.done.value)])
            POOL.wait([tok["k_ones", i]])

        def set_v_ones():
            for t_ in vl + vr:
                tok["v_ones",] = POOL.do(lambda e, t_=t_: e.memset(t_[:, :, :, D:VW], 1.0))

        def make_tables():
            PE.wait([tables])
            for i, (n0, n1) in enumerate(((0, HALF + P), (HALF + P, WIN))):
                tok["reltab",] = POOL.do(lambda e, i=i, n0=n0, n1=n1: e.tensor_tensor(
                    reltab[:, n0:n1, :], reltab[:, n0:n1, :],
                    relbase[:, i:i + 1, :].broadcast_to([P, n1 - n0, D]), ALU.subtract), [tables, reltab_loaded])
            bt_f, bt_p, bt_h = x1[1], x1[0], relout[0:SPLIT, 0, 0:PW // 2].bitcast(BF16)
            jobs = [(0, 0, GW, 0, 0), (0, GW, FW, 0, VOCAB - 1), (1, 0, FW, 0, 0), (1, FW, GW, HALF, VOCAB - 1)]
            for tab, c, n, r, base in jobs:
                prev = DVE.do(lambda e, c=c, n=n, r=r, base=base: e.tensor_scalar(
                    bt_f[0:SPLIT, c:c + n], embk6[:, r:r + n], embk6[:, base:base + 1], None, ALU.subtract),
                    [tables, (DVE.done, DVE.done.value)])
                if c == 0:
                    continue
                for part in range(3):
                    prev = DVE.do(lambda e, tab=tab: e.tensor_copy(bt_h, bt_f[0:SPLIT, 0:PW]), [prev])
                    keep = bandtab[tab]
                    if part == 0:
                        prev = DVE.do(lambda e, k=keep: e.tensor_scalar(
                            bt_p[0:SPLIT, 0:PW], bt_h, partmask[:, 0:1], None, ALU.mult), [prev])
                    else:
                        prev = DVE.do(lambda e, i=part: e.scalar_tensor_tensor(
                            bt_p[0:SPLIT, 0:PW], bt_h, partmask[:, i:i + 1],
                            bt_p[0:SPLIT, 0:PW], ALU.mult, ALU.add), [prev])
                    prev = DVE.do(lambda e: e.tensor_tensor(bt_f[0:SPLIT, 0:PW], bt_f[0:SPLIT, 0:PW],
                                                            bt_h, ALU.subtract), [prev])
                tok["bandtab",] = DVE.do(lambda e, k=keep: e.tensor_copy(k[:, :], bt_p[0:SPLIT, 0:PW]), [prev])
        def make_ternary():
            prev = DVE.do(lambda e: e.tensor_reduce(small[:, 0:1], wf[:], AX.XY, ALU.add, apply_absolute_value=True), [tables])
            i_, m, free = small_bank()
            prev = PE.do(lambda e: e.matmul(m[:, 0:1], ones, small[:, 0:1], start=True, stop=True),
                         [prev, ones_set, free])
            used["y"] = [prev]
            prev = DVE.do(lambda e: e.tensor_scalar(small[:, 1:2], m[:, 0:1], 1.0 / (H * H), 0.7, ALU.mult, ALU.mult), [prev])
            freed(i_, prev)
            prev = DVE.do(lambda e: e.tensor_scalar(small[:, 2:3], small[:, 1:2], -1.0, None, ALU.mult), [prev])
            above, below = zbuf[0], zbuf[1]
            for i in range(2):
                DVE.do(lambda e, i=i: e.tensor_scalar(above[:], wf[:, i, :], small[:, 1:2], None, ALU.is_gt), [prev])
                prev = DVE.do(lambda e, i=i: e.tensor_scalar(below[:], wf[:, i, :], small[:, 2:3], None, ALU.is_lt), [prev])
                prev = DVE.do(lambda e, i=i: e.tensor_tensor(above[:], above[:], below[:], ALU.subtract), [prev])
                tok["wf",] = prev = DVE.do(lambda e, i=i: e.tensor_scalar(wf[:, i, :], above[:], alpha[:, 0:1], None, ALU.mult), [prev])

        ln_used = [[] for _ in range(4)]

        def inv_std(k, srcs, after):
            n = len(srcs)
            r = rs[k]
            for i, s_ in enumerate(srcs):
                prev = DVE.do(lambda e, s_=s_, i=i: e.bn_stats(stats[k][:, i, :], s_), after + ln_used[k])
            for i in range(n):
                prev = DVE.do(lambda e, i=i: e.bn_aggr(mv[k][:, i, :], stats[k][:, i, :]), [prev])
            prev = DVE.do(lambda e: e.tensor_scalar(r[:, 0, 0:n], mv[k][:, 0:n, 1], EPS, None, ALU.add), [prev])
            v, h_, y, w_ = (r[:, j, 0:n] for j in range(4))
            POOL.do(lambda e: e.tensor_scalar(h_, v, -0.5, None, ALU.mult), [prev])
            prev = POOL.do(lambda e: e.tensor_scalar(y.bitcast(I32), v.bitcast(I32), -0.5, float(0x5f3759df),
                                                     ALU.mult, ALU.add))
            for _ in range(3):
                prev = POOL.do(lambda e: e.tensor_tensor(w_, y, y, ALU.mult), [prev])
                prev = POOL.do(lambda e: e.tensor_tensor(w_, w_, h_, ALU.mult), [prev])
                prev = POOL.do(lambda e: e.tensor_scalar(w_, w_, 1.5, None, ALU.add), [prev])
                prev = POOL.do(lambda e: e.tensor_tensor(y, y, w_, ALU.mult), [prev])
            return prev

        def normed(q, k, i, dst, src, after):
            tok = q.do(lambda e: e.tensor_scalar(dst, src, mv[k][:, i, 0:1], rs[k][:, 2, i:i + 1],
                                                 ALU.subtract, ALU.mult), after)
            ln_used[k] = [tok]
            return tok

        st = {"xc": [], "xnT": [], "qf": [], "qparts": [], "kparts": [], "qres": []}
        q_loaded, k_loaded, v_written, v_read = {}, {}, {}, {}
        chunk_written = {}

        def prep(b, c):
            buf = b % 2
            loc = {}

            helper = DVE if b == 0 else POOL

            xs = xc[:] if b else attn[:, c * CHUNK:(c + 1) * CHUNK, :]
            lnset = 0 if b else c

            def load_x():
                loc["x"] = SP.dma(xc[:], xrow[b, c], s_x, st["xc"])

            def normalise():
                loc["rs"] = inv_std(lnset, [xs[:, i, :] for i in range(CHUNK)], [loc["x"] if b else x0_loaded[c]])

            def normalised():
                for i in range(CHUNK):
                    loc["xn"] = normed(helper, lnset, i, xs[:, i, :], xs[:, i, :], [loc["rs"]])

            def transpose_x():
                i_, m, free = small_bank()
                for ih in range(2):
                    for i in range(CHUNK):
                        tr = PE.do(lambda e, ih=ih, i=i, m=m: e.matmul(
                            m[:, ih * CT + i * P:ih * CT + (i + 1) * P], xs[:, i, ih * P:(ih + 1) * P], ident[:],
                            start=True, stop=True, is_transpose=True), [loc["xn"], free, ident_loaded])
                st["xc"] = [tr]
                loc["xnT"] = ACTQ.do(lambda e, m=m: e.activation(xnT[:].rearrange("p i t -> p (i t)"), m[:, 0:2 * CT],
                                                                ACT.Copy), [tr] + st["xnT"])
                freed(i_, loc["xnT"])

            def project(w, bias, qp, used_):
                i_, m, free = small_bank()
                for g in range(G):
                    for ih in range(2):
                        mm = PE.do(lambda e, g=g, ih=ih, m=m: e.matmul(
                            m[:, g * CT:(g + 1) * CT], w[:, ih, g * P:(g + 1) * P], xnT[:, ih, :],
                            start=ih == 0, stop=ih == 1), [loc["xnT"], free, consts], signal=ih == 1)
                for g in range(G):
                    for dst, before in ((qf, st["qf"]), (qp[:, 0], st[used_])):
                        ev = ACTQ.do(lambda e, g=g, m=m, dst=dst: e.activation(
                            dst[:, g, :], m[:, g * CT:(g + 1) * CT], ACT.Identity, bias=bias[:, g:g + 1]), [mm] + before)
                freed(i_, ev)
                prev = helper.do(lambda e: e.tensor_tensor(qres[:], qf[:], qp[:, 0], ALU.subtract), [ev] + st["qres"])
                st["qf"] = [prev]
                prev = helper.do(lambda e: e.tensor_copy(qp[:, 1], qres[:]), [prev] + st[used_])
                prev = helper.do(lambda e: e.tensor_tensor(qp[:, 2], qres[:], qp[:, 1], ALU.subtract), [prev])
                st["qres"] = [prev]
                loc["split"] = prev
                return ev

            def write(qp, used_, parts, dram, rows, name):
                s_ = s_chunk[name][buf][c]
                for k in range(3):
                    at_ = [r for r in range(NB) if parts[r] == k]
                    step = at_[1] - at_[0] if len(at_) > 1 else 1
                    for g in range(G):
                        w_ = SP.dma(bass.AP(dram[buf].tensor, (g * rows + at_[0] * D) * HG * S + c * CT,
                                            [[S, P], [step * D * HG * S, len(at_)], [1, CT]]),
                                    qp[:, k, g:g + 1, :].broadcast_to([P, len(at_), CT]), s_,
                                    [loc["split"]] + chunk_reads(b - 2))
                st[used_] = [w_]
                chunk_written.setdefault((b, c), []).append(w_)

            def project_q():
                loc["q"] = project(wq, bq, qparts, "qparts")

            def write_q():
                write(qparts, "qparts", QPARTS, qd, QDROWS, "qd")

            def far_rows():
                i_, m, free = small_bank()
                mm = PE.do(lambda e, m=m: e.matmul(m[0:2 * HG, 0:G * CT], farw[:].rearrange("p a h -> p (a h)"),
                                                   qf[:].rearrange("p g t -> p (g t)"), start=True, stop=True),
                           [loc["q"], farw_ready, free])
                st["qf"] = st["qf"] + [mm]
                fv = qres[0:2 * HG, :, :]
                mv_ = m[0:2 * HG, 0:G * CT].rearrange("p (g t) -> p g t", g=G)
                cp = DVE.do(lambda e: e.tensor_copy(fparts[:, 0], mv_), [mm] + st["kparts"])
                ev = DVE.do(lambda e: e.tensor_tensor(fv, mv_, fparts[:, 0], ALU.subtract), [cp] + st["qres"])
                freed(i_, ev)
                cp = helper.do(lambda e: e.tensor_copy(fparts[:, 1], fv), [ev])
                loc["far"] = helper.do(lambda e: e.tensor_tensor(fparts[:, 2], fv, fparts[:, 1], ALU.subtract), [cp])
                st["qres"] = [loc["far"]]

            def write_far():
                for g in range(G):
                    w_ = SP.dma(bass.AP(qd[buf].tensor, (g * QDROWS + SPLIT) * HG * S + c * CT,
                                        [[S, 2 * HG], [2 * HG * S, 3], [1, CT]]), fparts[:, :, g, :],
                                s_chunk["far"][buf][c], [loc["far"]] + chunk_reads(b - 2))
                st["kparts"] = [w_]
                chunk_written[b, c].append(w_)

            def project_k():
                project(wk, bk, kparts, "kparts")

            def write_k():
                write(kparts, "kparts", KPARTS, kd, SPLIT, "kd")

            def project_v():
                i_, m, free = small_bank()
                for i in range(CHUNK):
                    for ih in range(2):
                        mm = PE.do(lambda e, i=i, ih=ih, m=m: e.matmul(
                            m[:, i * H:(i + 1) * H], xnT[:, ih, i * P:(i + 1) * P], wv[:, ih, :],
                            start=ih == 0, stop=ih == 1), [loc["xnT"], free], signal=ih == 1)
                for side, ring in enumerate((vl, vr)):
                    for g in range(G):
                        n = b * G + g
                        ev = DVE.do(lambda e, side=side, ring=ring, g=g, n=n, m=m: e.tensor_tensor(
                            ring[n % VRING][:, c * CHUNK:(c + 1) * CHUNK, :, 0:D].rearrange("p i h d -> p i h d"),
                            m[:, 0:CHUNK * H].rearrange("p (i g h d) -> p g i h d", i=CHUNK, g=G, h=HG)[:, g],
                            vbase[:, side:side + 1, g * P:(g + 1) * P].rearrange("p a (h d) -> p a h d", h=HG)
                            .broadcast_to([P, CHUNK, HG, D]), ALU.add),
                            [mm, vbase_ready] + v_read.get(n - VRING, []))
                        v_written[n] = [ev]
                freed(i_, ev)

            def xnT_free_after_v():
                project_v()
                xnT_free()

            def xnT_free():
                st["xnT"] = [(PE.done, PE.done.value)]

            if b == 0:
                return [(10 * c - 89.4, normalise), (10 * c - 85.5 if c else -89.3, normalised)] + [(c * 10 - 80 + i, f) for i, f in enumerate(
                    (transpose_x, project_q, far_rows, write_q, write_far, project_k, xnT_free_after_v, write_k))]
            return [(-7, load_x), (-5, normalise), (-5, normalised), (0, transpose_x), (1, project_q), (2, project_v),
                    (2.6, far_rows), (3.8, write_q), (5.6, project_k), (5.6, xnT_free), (4.6, write_far), (8.6, write_k)]

        def chunk_reads(b):
            if b < 0:
                return []
            return [q_loaded[s] for s in range(b * G * T, (b + 1) * G * T)][-QRING:] + \
                   [k_loaded[b * G + g, c] for g in range(G) for c in range(NCHUNK)]

        def get(*key):
            return [tok[key]] if key in tok else []

        def load_k(n, c):
            b, g = divmod(n, G)
            k_loaded[n, c] = SP.dma(ks[n % 2][0:SPLIT, :, c * CT:(c + 1) * CT], kd[b % 2][g, :, :, c * CT:(c + 1) * CT],
                                    s_ks[n % 2][c], chunk_written[b, c] + [tok["k_ones", n % 2]] + get("st_done", (n - 1) * T - 1))

        def load_q(s):
            n, t = divmod(s, T)
            b, g = divmod(n, G)
            i = s % QRING
            after = chunk_written[b, t // CHUNK] + get("st_done", s - QRING)
            src = qd[b % 2][g]
            for side in range(2):
                SP.dma(qs[i][0:SPLIT, side], src[0:SPLIT, :, t * P:(t + 1) * P], s_q[i], after)
                q_loaded[s] = SP.dma(qs[i][SPLIT:FAR, side],
                                     bass.AP(src.tensor, src.offset + (SPLIT + side) * HG * S + t * P,
                                             [[2 * HG * S, 3], [S, HG], [1, P]]), s_q[i], after)

        def band_raw(s, pair):
            i = s % QRING
            i_, m, free = small_bank()
            for j in range(2):
                h = 2 * pair + j
                for half in range(2):
                    mm = PE.do(lambda e, h=h, j=j, half=half, m=m: e.matmul(
                        m[HALF * half:HALF * (half + 1), j * PW:(j + 1) * PW],
                        ql[i][0:SPLIT, h, HALF * half:HALF * (half + 1)], bandtab[half][:], start=True, stop=True),
                        [q_loaded[s], tok["bandtab",], free], signal=j == 1)
            ev = ACTQ.do(lambda e, m=m: e.activation(praw[:, 2 * pair:2 * pair + 2, :].rearrange("p h c -> p (h c)"),
                                                     m[:, 0:2 * PW], ACT.Copy), [mm] + get("bw", s - 1))
            freed(i_, ev)
            tok["praw", s] = ev

        def band_write(s):
            k = s % 2
            for half, c0 in ((0, HALF), (1, P)):
                rows = slice(HALF * half, HALF * (half + 1))
                tok["bw", s] = SP.dma(bs[k].ap()[:, rows, c0:c0 + PW].rearrange("h p c -> p h c"), praw[rows, :, :],
                                      s_bw[k], [tok["praw", s]] + zeroed + get("br", s - 2))

        def band_read(s):
            k, i = s % 2, s % BRING
            after = [tok["bw", s]] + get("st_done", s - BRING)
            for half, c0, o, w in ((0, HALF, 0, HALF), (0, HALF + P, HALF, WIN - HALF),
                                   (1, HALF, 0, WIN - HALF), (1, HALF + WIN, WIN - HALF, HALF)):
                rows = slice(HALF * half, HALF * (half + 1))
                tok["br", s] = SP.dma(band[i][rows, :, o:o + w],
                                      bass.AP(bs[k], HALF * half * BROW + c0, [[BROW - 1, HALF], [P * BROW, HG], [1, w]]),
                                      s_br[i], after)

        def row_max(s, h):
            n, t = divmod(s, T)
            i, k, mx = s % QRING, ks[n % 2], maxes[s % 2]
            first = True
            kin = [k_loaded[n, c] for c in range(NCHUNK)] if t == 0 and h == 0 else []
            u = s * HG + h
            for c, key, length, side in score_pieces(t):
                after = [q_loaded[s]] + kin + get("max", u - 1, c // 512)
                last = c + length in (512, S)
                if side == "C":
                    for half, q_ in ((0, qr[i]), (1, ql[i])):
                        r = slice(HALF * half, HALF * (half + 1))
                        mm = PE.do(lambda e, r=r, q_=q_, c=c, key=key, length=length: e.matmul(
                            scores[r, c:c + length], q_[0:FAR, h, r], k[0:FAR, h, key:key + length],
                            start=True, stop=True), after, signal=last and half == 1)
                else:
                    q_ = ql[i] if side == "L" else qr[i]
                    mm = PE.do(lambda e, q_=q_, c=c, key=key, length=length: e.matmul(
                        scores[:, c:c + length], q_[0:FAR, h, :], k[0:FAR, h, key:key + length],
                        start=True, stop=True), after, signal=last)
                if c + length == 512:
                    full0 = mm
            width, off = window(t)
            mxfree = get("negmax", s - 2)
            DVE.do(lambda e: e.tensor_tensor_reduce(
                junk[:, 0:width], scores[:, 0:width], band[s % BRING][:, h, off:off + width], 1.0, LOWEST,
                ALU.add, ALU.max, mx[:, h, 0:1]), [full0, tok["br", s]] + mxfree + get("max", u - 1, 1) )
            tok["max", u, 0] = DVE.do(lambda e: e.tensor_reduce(mx[:, h, 1:2], scores[:, width:512], AX.X, ALU.max))
            tok["max", u, 1] = DVE.do(lambda e: e.tensor_reduce(mx[:, h, 2:3], scores[:, 512:S], AX.X, ALU.max), [mm])

        def max_reduce(s):
            tok["negmax", s] = DVE.do(lambda e: e.tensor_reduce(negmax[s % 2][:], maxes[s % 2][:], AX.X, ALU.max, negate=True),
                                      [tok["max", s * HG + HG - 1, 1]] + get("nmT", s - 2))

        def max_rows(s):
            i_, m, free = small_bank()
            tr = PE.do(lambda e, m=m: e.matmul(m[0:HG, 0:P], negmax[s % 2][:], ident[:], start=True, stop=True,
                                               is_transpose=True), [tok["negmax", s], free])
            tok["nmT", s] = tr
            c1 = DVE.do(lambda e, m=m: e.tensor_copy(nm[:, 0], m[0:HG, 0:P]), [tr] + get("nmw", s - 1))
            tok["nm2", s] = DVE.do(lambda e, m=m: e.tensor_tensor(nm[:, 1], m[0:HG, 0:P], nm[:, 0], ALU.subtract), [c1])
            freed(i_, tok["nm2", s])

        def max_write(s):
            tok["nmw", s] = SP.dma(nmd[s % 2].ap().rearrange("r h q -> h r q"), nm[:], s_nmw[s % 2], [tok["nm2", s]] + get("nm", s - 2))

        def max_read(s):
            tok["nm", s] = SP.dma(qs[s % QRING][FAR:ROWS].rearrange("r a h q -> r a (h q)"),
                                  bass.AP(nmd[s % 2], 0, [[HG * P, 2], [0, 2], [1, HG * P]]), s_nm[s % 2],
                                  [tok["nmw", s]] + get("st_done", s - QRING))

        bankT = {"n": 0}
        exp_tok = {}

        def weights(s, h, kind):
            n, t = divmod(s, T)
            i, k = s % QRING, ks[n % 2]
            tiles = tile_layout(t)[0 if kind == "X" else 1]
            j = bankT["n"] % 3
            bankT["n"] += 1
            m = logitsT[j]
            after = [tok["nm", s], q_loaded[s]] + get("exp", bankT["n"] - 4)
            for c, kt in enumerate(tiles):
                lhs = k[0:ROWS, h, kt * P:(kt + 1) * P]
                band_tile = kind == "X" and abs(kt - t) <= 1
                last = c == len(tiles) - 1
                if kt == t:
                    for half, q_ in ((0, qr[i]), (1, ql[i])):
                        mm = PE.do(lambda e, c=c, half=half, q_=q_, lhs=lhs: e.matmul(
                            m[:, c * P + HALF * half:c * P + HALF * (half + 1)], lhs,
                            q_[0:ROWS, h, HALF * half:HALF * (half + 1)], start=half == 0, stop=not band_tile,
                            skip_group_check=True), after, signal=False)
                else:
                    q_ = ql[i] if kt < t else qr[i]
                    mm = PE.do(lambda e, c=c, q_=q_, lhs=lhs: e.matmul(
                        m[:, c * P:(c + 1) * P], lhs, q_[0:ROWS, h, :], start=True, stop=not band_tile,
                        skip_group_check=True), after, signal=last and not band_tile)
                if band_tile:
                    if kt < t:
                        src, idn = band[s % BRING][0:HALF, h, 0:HALF], ident[0:HALF, 0:HALF]
                        dst = m[HALF:P, c * P:c * P + HALF]
                    elif kt == t:
                        src, idn, dst = band[s % BRING][:, h, HALF:HALF + P], ident[:], m[:, c * P:(c + 1) * P]
                    else:
                        src, idn, dst = band[s % BRING][:, h, HALF + P:WIN], ident[:], m[0:HALF, c * P:(c + 1) * P]
                    mm = PE.do(lambda e, src=src, idn=idn, dst=dst, kt=kt: e.matmul(
                        dst, src, idn, start=False, stop=True, is_transpose=kt >= t, skip_group_check=True),
                        [tok["br", s]], signal=last)
            tok["st_done", s] = mm
            if kind == "X":
                ACTQ.do(lambda e: e.activation(wx[:, s % 2, h, :], m[:, 0:NEAR], ACT.Exp),
                        [mm] + get("rel", s // 2 - 1) + get("pvX", s - 2, h // 4))
                dst, src = wr[:, h % 4, :], m[:, NEAR:512]
                free = get("pvX", s - 1, 1) if h < 4 else get("pvX", s, 0)
            else:
                dst, src = wy[:, h % 4, :], m[:]
                free = get("pvY", s - 1, 1) if h < 4 else get("pvY", s, 0)
            e_ = ACTQ.do(lambda e: e.activation(dst, src, ACT.Exp), [mm] + free)
            tok["exp", bankT["n"] - 1] = e_
            exp_tok[s, h, kind] = e_

        def weighted(s, blk, kind):
            n, t = divmod(s, T)
            tiles = tile_layout(t)[0 if kind == "X" else 1]
            VL, VR = vl[n % VRING], vr[n % VRING]
            after = [exp_tok[s, 4 * blk + j, kind] for j in range(4)] + v_written[n] + [tok["v_ones",]]
            first = s % 2 == 0 and blk == 0 and kind == "X"
            if first:
                after = after + get("o_out", s // 2 - 1)
            o0 = (s % 2 * 2 + blk) * P
            for c, kt in enumerate(tiles):
                for j in range(4):
                    h = 4 * blk + j
                    V = VL if kt <= t else VR
                    if kind == "Y":
                        src = wy[:, j, c * P:(c + 1) * P]
                    else:
                        src = wr[:, j, :] if c == 3 else wx[:, s % 2, h, c * P:(c + 1) * P]
                    mm = PE.do(lambda e, V=V, h=h, j=j, c=c, kt=kt, src=src: e.matmul(
                        oacc[32 * j:32 * j + VW, o0:o0 + P], V[:, kt, h, :], src,
                        start=first and c == 0, stop=True, skip_group_check=True),
                        after, signal=c == len(tiles) - 1 and j == 3)
            tok["pv" + kind, s, blk] = mm
            if kind == "Y" and blk == 1:
                v_read[n] = [mm]
                tok["pv_all", s] = mm

        RG = 512 // (2 * HG * QG)
        rel_bank = []

        def relative(pair, part, piece):
            t = 2 * pair % T
            if piece == 0:
                rel_bank[:] = small_bank()
                bank["held"] = rel_bank[0]
            i_, m, free = rel_bank
            after = [exp_tok[2 * pair + j, h, "X"] for j in range(2) for h in range(HG)] + [free, tok["reltab",]]
            for gq in range(piece * RG // 2, (piece + 1) * RG // 2):
                q0 = (part * RG + gq) * QG
                side = -1 if q0 < HALF else 1
                has = [j for j in range(2) if 0 <= t + j + side < T]
                for off, js in ((0, [0, 1]), (side, has)):
                    n0 = P * off - (q0 + QG - 1) + (EXT // 2)
                    c = (1 + off) * P + q0
                    j0, j1 = js[0], js[-1] + 1
                    o0 = (gq * 2 + j0) * HG * QG
                    mm = PE.do(lambda e, n0=n0, c=c, j0=j0, j1=j1, o0=o0, m=m, off=off: e.matmul(
                        m[:, o0:o0 + (j1 - j0) * HG * QG], reltab[:, n0:n0 + QG, :].rearrange("p n d -> p (n d)"),
                        wx[:, j0:j1, :, c:c + QG], start=off == 0, stop=off != 0, skip_group_check=True),
                        after, signal=gq == RG - 1 and off != 0)
            if piece == 0:
                return
            bank["held"] = None
            tok["rel", pair] = mm
            if part == 2:
                relative_sum(pair, 0)
            ev = DVE.do(lambda e, m=m: e.tensor_tensor(
                relout[:, part % 2, :].rearrange("p (a c) -> p a c", c=QG), m[:].rearrange("p (a c) -> p a c", c=QG),
                relmask[:].rearrange("p (a c) -> p a c", a=1).broadcast_to([P, 512 // QG, QG]), ALU.mult),
                [mm] + get("relsum_last"))
            freed(i_, ev)
            tok["relout", pair, part] = ev

        def relative_sum(pair, half):
            src = relout[:].rearrange("p a (g j h c) -> p (a g) j h c", j=2, h=HG, c=QG)
            for st_ in range(2):
                for blk in range(2):
                    o0 = (st_ * 2 + blk) * P + half * HALF
                    for j in range(4):
                        mm = PE.do(lambda e, st_=st_, h=4 * blk + j, j=j, o0=o0: e.matmul(
                            oacc[32 * j:32 * j + D, o0:o0 + HALF], relsum[:], src[:, :, st_, h, :],
                            start=False, stop=True, skip_group_check=True),
                            [tok["relout", pair, 2 * half + 1]], signal=st_ == 1 and blk == 1 and j == 3)
            tok["relsum_last",] = mm

        def out_copy(pair):
            tok["o_out", pair] = ACTQ.do(lambda e: e.activation(oT[:].rearrange("p j a q -> p (j a q)"), oacc[:], ACT.Copy),
                                         [tok["pv_all", 2 * pair + 1], tok["relsum_last",]] + get("o_tr", 2 * pair - 1))

        def out_norm(s):
            n, t = divmod(s, T)
            b, g = divmod(n, G)
            i_, m, free = small_bank()
            for blk in range(2):
                tr = PE.do(lambda e, blk=blk, m=m: e.matmul(m[:, blk * P:(blk + 1) * P], oT[:, s % 2, blk, :], ident[:],
                                                            start=True, stop=True, is_transpose=True),
                           [tok["o_out", s // 2], free])
            tok["o_tr", s] = tr
            view = m[:, 0:2 * P].rearrange("p (h c) -> p h c", c=32)
            rc = DVE.do(lambda e: e.reciprocal(rsum[:], view[:, :, D]), [tr] + get("norm", s - 1))
            ev = DVE.do(lambda e: e.tensor_tensor(
                attn[:, t, g * P:(g + 1) * P].rearrange("p (h d) -> p h d", d=D), view[:, :, 0:D],
                rsum[:].rearrange("p (h o) -> p h o", o=1).broadcast_to([P, HG, D]), ALU.mult),
                [rc] + get("att_read", b - 1, t))
            freed(i_, ev)
            tok["norm", s] = ev

        xtile = a["x"].rearrange("(n p) h -> n p h", p=P)
        otile = out.rearrange("(n p) h -> n p h", p=P)
        last_tile = {}

        def tail_load(b, t):
            r = b * T + t
            tok["xt", r] = SP.dma(x1[r % 2][:], xtile[r], s_xt[r % 2], [tok["bandtab",]] + get("z", r - 2))

        def transposed(src, after):
            i_, m, free = small_bank()
            for ih in range(2):
                tr = PE.do(lambda e, ih=ih, m=m: e.matmul(m[:, ih * P:(ih + 1) * P], src[:, ih * P:(ih + 1) * P], ident[:],
                                                          start=True, stop=True, is_transpose=True), after + [free])
            ev = ACTQ.do(lambda e, m=m: e.activation(rowsT[:].rearrange("p i t -> p (i t)"), m[:, 0:H], ACT.Copy),
                         [tr] + used["rowsT"])
            freed(i_, ev)
            return tr, ev

        def linear(w, bias, dst, after, dst_free):
            i_, m, free = small_bank()
            for ih in range(2):
                mm = PE.do(lambda e, ih=ih, m=m: e.matmul(m[:, 0:H], rowsT[:, ih, :], w[:, ih, :], start=ih == 0, stop=ih == 1),
                           after + [free], signal=ih == 1)
            ev = DVE.do(lambda e, m=m: e.tensor_tensor(dst[:], m[:, 0:H], bias[:], ALU.add), [mm] + dst_free)
            freed(i_, ev)
            used["rowsT"] = [mm]
            return ev

        def tail_attT(b, t):
            r = b * T + t
            tok["att_read", b, t], tok["attT", r] = transposed(attn[:, t, :], [tok["norm", (b * G + 1) * T + t]])

        def tail_wo(b, t):
            r = b * T + t
            ev = linear(wo, bo, ybuf, [tok["attT", r]], used["y"])
            tok["iy", r] = inv_std(1, [ybuf[:]], [ev])

        def tail_x1(b, t):
            r = b * T + t
            yn = normed(DVE, 1, 0, ybuf[:], ybuf[:], [tok["iy", r]])
            tok["x1", r] = POOL.do(lambda e: e.tensor_tensor(x1[r % 2][:], ybuf[:], x1[r % 2][:], ALU.add),
                                   [yn, tok["xt", r]])
            used["y"] = [tok["x1", r]]

        def tail_norm(b, t):
            r = b * T + t
            tok["ix", r] = inv_std(2, [x1[r % 2][:]], [tok["x1", r]])

        def tail_normed(b, t):
            r = b * T + t
            tok["xn1", r] = normed(DVE, 2, 0, zbuf[r % 2][:], x1[r % 2][:], [tok["ix", r]] + get("stored", r - 2))

        def tail_x1T(b, t):
            r = b * T + t
            _, tok["x1T", r] = transposed(zbuf[r % 2], [tok["xn1", r]])

        def tail_ff(b, t):
            r = b * T + t
            z = zbuf[r % 2]
            ev = linear(wf, bf, z, [tok["x1T", r], tok["wf",]], get("stored", r - 2))
            tok["iz", r] = inv_std(3, [z[:]], [ev])

        def tail_out(b, t):
            r = b * T + t
            z = zbuf[r % 2]
            zn = normed(DVE, 3, 0, z[:], z[:], [tok["iz", r]])
            tok["z", r] = POOL.do(lambda e: e.tensor_tensor(z[:], z[:], x1[r % 2][:], ALU.add), [zn])

        def tail_store(b, t):
            r = b * T + t
            last_tile[r % 2] = tok["stored", r] = SP.dma(otile[r], zbuf[r % 2][:], s_out[r % 2], [tok["z", r]])

        todo = {}

        def at(slot, f, *args):
            todo.setdefault(slot, []).append((f, args))

        at(-88, set_k_ones, 0)
        at(-30, set_k_ones, 1)
        at(-71, set_v_ones)
        at(-42.5, make_tables)
        at(-12, make_ternary)
        for b in range(B):
            for c in range(NCHUNK):
                first = ((b - 1) * G * T + T + c) * HG + 12 if b else 0
                for x, stage in prep(b, c):
                    at(first + x, stage)
        for s in range(STEPS):
            n, t = divmod(s, T)
            b, g = divmod(n, G)
            pair, odd = divmod(s, 2)
            z = pair * 2 * HG
            w0 = z + 5.6 * odd
            m0 = z - 13.8 + 7.8 * odd
            if t == 0:
                for c in range(NCHUNK):
                    at(z - 41.8 + (8 * c if n else 0), load_k, n, c)
            at(m0 - 10.5 if s >= QRING else -42, load_q, s)
            for heads in range(HG // 2):
                at(m0 - 8 + 0.7 * heads, band_raw, s, heads)
            at(m0 - 5.3, band_write, s)
            at(m0 - 3.9, band_read, s)
            for h in range(HG):
                at(m0 + 0.97 * h, row_max, s, h)
            at(m0 + 7.3, max_reduce, s)
            at(m0 + 8.3, max_rows, s)
            at(m0 + 8.35, max_write, s)
            at(m0 + 9.1, max_read, s)
            for blk in range(2):
                o = w0 + 2.8 * blk
                for j in range(4):
                    at(o + 0.35 * j, weights, s, 4 * blk + j, "X")
                    at(o + 1.4 + 0.35 * j, weights, s, 4 * blk + j, "Y")
                at(o + 1.96, weighted, s, blk, "X")
                at(o + 3.36, weighted, s, blk, "Y")
            if odd:
                for part in range(4):
                    at(z + 11.2 + 1.1 * part, relative, pair, part, 0)
                    at(z + 11.75 + 1.1 * part, relative, pair, part, 1)
                at(z + 16.45, relative_sum, pair, 1)
                at(z + 16.5, out_copy, pair)
                at(z + 17.3, out_norm, s - 1)
                at(z + 17.6, out_norm, s)
            if g == 1:
                o = s * HG + T * HG + 3 if b < B - 1 else z + 18 + 3 * odd
                for x, f in ((-3, tail_load), (0, tail_attT), (0.8, tail_wo), (3, tail_x1), (4, tail_norm),
                             (6.2, tail_normed), (7.3, tail_x1T), (8, tail_ff), (10.4, tail_out), (11.6, tail_store)):
                    at(o + x, f, b, t)
        for slot in sorted(todo):
            for f, args in todo[slot]:
                f(*args)
        SP.wait([last_tile[0], last_tile[1]])

        with nc.Block() as block:
            @block.sync
            def _(e):
                SP.run(e)

            @block.gpsimd
            def _(e):
                POOL.run(e)

            @block.tensor
            def _(e):
                PE.run(e)

            @block.vector
            def _(e):
                DVE.run(e)

            @block.scalar
            def _(e):
                ACTQ.run(e)


def kernel(L0_attn_x, L0_attn_mask, L0_attn_Wq, L0_attn_bq, L0_attn_Wk, L0_attn_bk, L0_attn_Wv, L0_attn_bv, L0_attn_Wo,
           L0_attn_bo, L0_attn_embK, L0_attn_embV, L0_ffn_weight, L0_ffn_alpha, L0_ffn_bias):
    from concourse import bacc
    from concourse.bass_utils import run_bass_kernel_spmd

    def arr(v):
        return np.asarray(v)

    order = np.arange(H).reshape(G, HG, D).transpose(0, 2, 1).reshape(-1)
    embK, embV = arr(L0_attn_embK), arr(L0_attn_embV)
    near = np.clip(np.arange(EXT) - EXT // 2, -MRP, MRP) + MRP
    p = np.arange(P)
    f32 = np.float32
    ins = {
        "x": arr(L0_attn_x).reshape(B * S, H),
        "WqT": arr(L0_attn_Wq).T[:, order], "WkT": arr(L0_attn_Wk).T[:, order],
        "WvT": arr(L0_attn_Wv).T, "WoT": arr(L0_attn_Wo).T, "WfT": arr(L0_ffn_weight).T,
        "bq": arr(L0_attn_bq)[order].reshape(G, P).T, "bk": arr(L0_attn_bk)[order].reshape(G, P).T,
        "bv": arr(L0_attn_bv), "bo": arr(L0_attn_bo), "bf": arr(L0_ffn_bias), "alpha": arr(L0_ffn_alpha),
        "efarV": np.stack([np.tile(embV[0], NH), np.tile(embV[-1], NH)]),
        "relbase": np.stack([embV[0], embV[-1]]),
        "extV": embV[near].reshape(-1),
        "kfar": np.stack([np.repeat(embK[0], HG), np.repeat(embK[-1], HG)], axis=1),
        "embk6": np.tile(embK.T, (NB, 1)),
        "ident": np.eye(P, dtype=f32),
        "headmask": (p[:, None] % HG == np.arange(HG)).astype(f32),
        "relmask": (QG - 1 - p[:, None] // D == np.arange(QG)).astype(f32),
        "relsum": (p[:, None] % D == np.arange(D)).astype(f32),
        "partmask": (np.repeat(KPARTS, D)[:, None] == np.arange(3)).astype(f32),
    }
    nc = bacc.Bacc("TRN2", target_bir_lowering=False, num_devices=1)
    aps = {}
    for k in ins:
        ins[k] = np.ascontiguousarray(ins[k])
        aps[k] = nc.dram_tensor("in_" + k, ins[k].shape, mybir.dt.from_np(ins[k].dtype), kind="ExternalInput").ap()
    out = nc.dram_tensor("out", (B * S, H), F32, kind="ExternalOutput").ap()
    build(nc, aps, out)
    r = run_bass_kernel_spmd(nc, [{"in_" + k: v for k, v in ins.items()}], core_ids=[0])
    return r.results[0]["out"].reshape(B, S, H)
```
